# Optimizing a Trainium2 kernel written in Bass

```python
import numpy as np
import jax
import jax.numpy as jnp

def _softmax(x, axis=-1):
    return jax.nn.softmax(x, axis=axis)

def _gelu(x):
    return jax.nn.gelu(x, approximate=True)

def _silu(x):
    return jax.nn.silu(x)

def _sigmoid(x):
    return jax.nn.sigmoid(x)

def _layernorm(x, axis=-1, eps=1e-05):
    m = jnp.mean(x, axis=axis, keepdims=True)
    v = jnp.var(x, axis=axis, keepdims=True)
    return (x - m) / jnp.sqrt(v + eps)

def _scatter_add(tgt, idx, src, axis=0):
    return tgt.at[idx].add(src)

def _segment_sum(src, seg, n):
    return jax.ops.segment_sum(src, seg, n)
kernel_name = 'mk_gnn_resnorm_d2_gnn_r16_7bcd58'

def setup_inputs(seed: int=0):
    np.random.seed(seed)
    _w = jnp.asarray

    def _rec_inputs():
        import jax
        import jax.numpy as jnp
        _gk = jax.random.key(seed)
        x = -6.415e-05 + 1 * jax.random.normal(jax.random.fold_in(_gk, 1), (3125, 512), jnp.float32)
        _s = jax.random.randint(jax.random.fold_in(_gk, 2), (25000,), 0, 3125, jnp.int32)
        _d = jax.random.randint(jax.random.fold_in(_gk, 3), (25000,), 0, 3125, jnp.int32)
        _loop = jnp.arange(3125, dtype=jnp.int32)
        src = jnp.concatenate([_s, _d, _loop])
        dst = jnp.concatenate([_d, _s, _loop])
        _o = jnp.argsort(dst, stable=True)
        src = src[_o]
        dst = dst[_o]
        edge_attr_20 = 0.000389844 + 1.00025 * jax.random.normal(jax.random.fold_in(_gk, 12), (53125, 20), jnp.float32)
        edge_attr_4 = -0.00185629 + 0.998788 * jax.random.normal(jax.random.fold_in(_gk, 13), (53125, 4), jnp.float32)
        edge_weight = jax.random.uniform(jax.random.fold_in(_gk, 14), (53125,), jnp.float32, 0.0, 0.999993)
        return (x, src, dst, edge_attr_20, edge_attr_4, edge_weight)
    x, src, dst, edge_attr_20, edge_attr_4, edge_weight = _rec_inputs()

    def _L0_gnn_setup():
        import jax, jax.numpy as jnp
        import numpy as np
        N_NODES = 1250
        N_EDGES = 20000
        D = 512
        L = 3
        key = jax.random.key(seed)
        ks = jax.random.split(key, 6)
        x = jax.random.normal(ks[0], (N_NODES, D), dtype=jnp.float32)
        Ws_self = jax.random.normal(ks[1], (L, D, D), dtype=jnp.float32) * 0.05
        Ws_neigh = jax.random.normal(ks[2], (L, D, D), dtype=jnp.float32) * 0.05
        bs = jax.random.normal(ks[3], (L, D), dtype=jnp.float32) * 0.05
        src = jax.random.randint(ks[4], (N_EDGES,), 0, N_NODES, dtype=jnp.int64)
        dst = jax.random.randint(ks[5], (N_EDGES,), 0, N_NODES, dtype=jnp.int64)
        return {'x': x, 'Ws_self': Ws_self, 'Ws_neigh': Ws_neigh, 'bs': bs, 'src': src, 'dst': dst}
    _L0_gnn_all = _L0_gnn_setup()
    _L0_gnn_in = {k: v for k, v in _L0_gnn_all.items() if k in ('Ws_self', 'Ws_neigh', 'bs')}
    del _L0_gnn_all

    def _L1_gnn_setup():
        import jax, jax.numpy as jnp
        import numpy as np
        import math
        B = 128
        F = 32
        R = 20
        N = 1024
        E = 16384
        LOG2 = 0.6931471805599453
        IS2 = 1.0 / math.sqrt(2.0)
        IS3 = 1.0 / math.sqrt(3.0)
        IS6 = 1.0 / math.sqrt(6.0)

        def ssp(x):
            return jax.nn.softplus(x) - LOG2
        key = jax.random.key(seed)
        ks = jax.random.split(key, 14)
        return dict(x=jax.random.normal(ks[0], (N, 4 * B), jnp.float32), idx_i=jax.random.randint(ks[1], (E,), 0, N), idx_j=jax.random.randint(ks[2], (E,), 0, N), f_ij=jax.random.normal(ks[3], (E, R), jnp.float32), rcut_ij=jax.random.uniform(ks[4], (E,), jnp.float32), Yr_ij=jax.random.normal(ks[5], (E, 4), jnp.float32), w_in2f_s=jax.random.normal(ks[6], (B, F), jnp.float32), w_in2f_v=jax.random.normal(ks[7], (B, F), jnp.float32), W1=jax.random.normal(ks[8], (R, F), jnp.float32) / math.sqrt(R), b1=jnp.zeros((F,), jnp.float32), W2=jax.random.normal(ks[9], (F, 6 * F), jnp.float32) / math.sqrt(F), b2=jnp.zeros((6 * F,), jnp.float32), w_f2o1_s=jax.random.normal(ks[10], (2 * F, B), jnp.float32), w_f2o1_v=jax.random.normal(ks[11], (2 * F, B), jnp.float32), w_f2o2_s=jax.random.normal(ks[12], (B, B), jnp.float32), w_f2o2_v=jax.random.normal(ks[13], (B, B), jnp.float32))
    _L1_gnn_all = _L1_gnn_setup()
    _L1_gnn_in = {k: v for k, v in _L1_gnn_all.items() if k in ('w_in2f_s', 'w_in2f_v', 'W1', 'b1', 'W2', 'b2', 'w_f2o1_s', 'w_f2o1_v', 'w_f2o2_s', 'w_f2o2_v')}
    del _L1_gnn_all
    return {'x': x, 'src': src, 'dst': dst, 'edge_attr_20': edge_attr_20, 'edge_attr_4': edge_attr_4, 'edge_weight': edge_weight, 'L0_gnn_Ws_self': _L0_gnn_in['Ws_self'], 'L0_gnn_Ws_neigh': _L0_gnn_in['Ws_neigh'], 'L0_gnn_bs': _L0_gnn_in['bs'], 'L1_gnn_w_in2f_s': _L1_gnn_in['w_in2f_s'], 'L1_gnn_w_in2f_v': _L1_gnn_in['w_in2f_v'], 'L1_gnn_W1': _L1_gnn_in['W1'], 'L1_gnn_b1': _L1_gnn_in['b1'], 'L1_gnn_W2': _L1_gnn_in['W2'], 'L1_gnn_b2': _L1_gnn_in['b2'], 'L1_gnn_w_f2o1_s': _L1_gnn_in['w_f2o1_s'], 'L1_gnn_w_f2o1_v': _L1_gnn_in['w_f2o1_v'], 'L1_gnn_w_f2o2_s': _L1_gnn_in['w_f2o2_s'], 'L1_gnn_w_f2o2_v': _L1_gnn_in['w_f2o2_v']}

def reference(x, src, dst, edge_attr_20, edge_attr_4, edge_weight, L0_gnn_Ws_self, L0_gnn_Ws_neigh, L0_gnn_bs, L1_gnn_w_in2f_s, L1_gnn_w_in2f_v, L1_gnn_W1, L1_gnn_b1, L1_gnn_W2, L1_gnn_b2, L1_gnn_w_f2o1_s, L1_gnn_w_f2o1_v, L1_gnn_w_f2o2_s, L1_gnn_w_f2o2_v):
    import jax
    import jax.numpy as jnp

    def _L0_gnn_ref(x, Ws_self, Ws_neigh, bs, src, dst):
        import jax, jax.numpy as jnp
        import numpy as np
        N_NODES = 1250
        N_EDGES = 20000
        D = 512
        L = 3
        n = x.shape[0]
        deg = jax.ops.segment_sum(jnp.ones_like(dst, dtype=x.dtype), dst, num_segments=n)
        inv_deg = (1.0 / jnp.clip(deg, 1.0))[:, None]
        h = x
        n_layers = Ws_self.shape[0]
        for l in range(n_layers):
            neigh = jax.ops.segment_sum(h[src], dst, num_segments=n) * inv_deg
            h = h @ Ws_self[l] + neigh @ Ws_neigh[l] + bs[l]
            if l != n_layers - 1:
                h = jax.nn.relu(h)
        return h

    def _L1_gnn_ref(x, idx_i, idx_j, f_ij, rcut_ij, Yr_ij, w_in2f_s, w_in2f_v, W1, b1, W2, b2, w_f2o1_s, w_f2o1_v, w_f2o2_s, w_f2o2_v):
        import jax, jax.numpy as jnp
        import numpy as np
        import math
        B = 128
        F = 32
        R = 20
        N = 1024
        E = 16384
        LOG2 = 0.6931471805599453
        IS2 = 1.0 / math.sqrt(2.0)
        IS3 = 1.0 / math.sqrt(3.0)
        IS6 = 1.0 / math.sqrt(6.0)

        def ssp(x):
            return jax.nn.softplus(x) - LOG2
        n = x.shape[0]
        xs = x[:, :B]
        xv = x[:, B:].reshape(n, B, 3)
        hs = xs @ w_in2f_s / math.sqrt(B)
        hv = jnp.einsum('nbc,bf->nfc', xv, w_in2f_v) / math.sqrt(B)
        s = hs[idx_j]
        v = hv[idx_j]
        ys = Yr_ij[:, 0]
        yv = Yr_ij[:, 1:4]
        t_s1 = s * ys[:, None]
        t_s2 = jnp.einsum('efc,ec->ef', v, yv) * IS3
        t_v1 = s[:, :, None] * yv[:, None, :]
        t_v2 = v * ys[:, None, None]
        t_pv = jnp.cross(v, yv[:, None, :]) * IS2
        ax, ay, az = (v[..., 0], v[..., 1], v[..., 2])
        bx, by, bz = (yv[:, None, 0:1], yv[:, None, 1:2], yv[:, None, 2:3])
        bx, by, bz = (bx[..., 0], by[..., 0], bz[..., 0])
        t_q = jnp.stack([(ax * by + ay * bx) * IS2, (ay * bz + az * by) * IS2, (2.0 * az * bz - ax * bx - ay * by) * IS6, (ax * bz + az * bx) * IS2, (ax * bx - ay * by) * IS2], axis=-1)
        h = ssp(f_ij @ W1 + b1)
        Wij = (h @ W2 + b2) * rcut_ij[:, None]
        Wf = Wij.reshape(-1, F, 6)
        edge = jnp.concatenate([(t_s1 * Wf[..., 0])[..., None], (t_s2 * Wf[..., 1])[..., None], t_v1 * Wf[..., 2:3], t_v2 * Wf[..., 3:4], t_pv * Wf[..., 4:5], t_q * Wf[..., 5:6]], axis=-1)
        agg = jax.ops.segment_sum(edge.reshape(edge.shape[0], -1), idx_i, num_segments=n).reshape(n, F, 16)
        s_in = jnp.concatenate([agg[..., 0], agg[..., 1]], axis=1)
        v_in = jnp.concatenate([agg[..., 2:5], agg[..., 5:8]], axis=1)
        os1 = s_in @ w_f2o1_s / math.sqrt(2 * F)
        ov1 = jnp.einsum('nmc,mb->nbc', v_in, w_f2o1_v) / math.sqrt(2 * F)
        os1 = ssp(os1)
        os2 = os1 @ w_f2o2_s / math.sqrt(B)
        ov2 = jnp.einsum('nbc,bd->ndc', ov1, w_f2o2_v) / math.sqrt(B)
        return jnp.concatenate([os2, ov2.reshape(n, -1)], axis=-1)
    x = _layernorm(x + _L0_gnn_ref(x, L0_gnn_Ws_self, L0_gnn_Ws_neigh, L0_gnn_bs, src, dst), axis=-1)
    x = _layernorm(x + _L1_gnn_ref(x, src, dst, edge_attr_20, edge_weight, edge_attr_4, L1_gnn_w_in2f_s, L1_gnn_w_in2f_v, L1_gnn_W1, L1_gnn_b1, L1_gnn_W2, L1_gnn_b2, L1_gnn_w_f2o1_s, L1_gnn_w_f2o1_v, L1_gnn_w_f2o2_s, L1_gnn_w_f2o2_v), axis=-1)
    return x

_drawn_inputs = setup_inputs


def setup_inputs(seed=0):
    import zlib

    import numpy as np

    out = dict(_drawn_inputs(seed))
    spreads = {'L1_gnn_b1': (0.0, 0.1), 'L1_gnn_b2': (0.0, 0.1)}
    factors = {}
    for name, (base, spread) in spreads.items():
        noise = np.random.default_rng([zlib.crc32(name.encode()), seed]).standard_normal(out[name].shape)
        drawn = base * np.exp(spread * noise) if base else spread * noise
        out[name] = jnp.asarray(drawn.astype(out[name].dtype))
    for name, factor in factors.items():
        out[name] = (out[name] * factor).astype(out[name].dtype)
    return out
```

```python
import concourse.bass as bass
from concourse import mybir

F32 = mybir.dt.float32
F16 = mybir.dt.float16
BF16 = mybir.dt.bfloat16
I32 = mybir.dt.int32
ALU = mybir.AluOpType
ACT = mybir.ActivationFunctionType
AX = mybir.AxisListType

P = 128
N, E, D = 3125, 53125, 512
TILES = 25
TN = N // TILES
SLOTS = -(-E // (TILES * P)) + 1
WIN = P * SLOTS
LAYERS = 3
PASSES = LAYERS + 1
EP = 125
EC = E // EP
BLK = 5
NB = EC // BLK
MAXR = -(-E // WIN)
ROUND_MAX = PASSES * TILES * MAXR + 2
BIG = float(1 << 20)
KC = D // P
B, F, R, YD, C3 = 128, 32, 20, 4, 3
PAY_Y, PAY_C, PAY_SRC, PAY_DST, PAY = R, R + YD, R + YD + 1, R + YD + 2, R + YD + 4
CH = -(-E // P)
BINS = TILES + 1
PIECE = 16
PIECES = CH // PIECE
CB = -(-CH // P)
G = 4 * F
HI, LO, SC, ISC, ROW = 0, D, 2 * D, 2 * D + 2, 2 * D + 4
LOG2 = 0.6931471805599453
EPS = 1e-5
HALF = SLOTS // 2


class Chain:

    def __init__(self, engine, sem, base=0):
        self.engine, self.sem, self.base, self.k = engine, sem, base, 0

    def link(self, ins):
        self.k += 1
        ins.then_inc(self.sem, 1)
        self.engine.wait_ge(self.sem, self.base + self.k)


def gnn_kernel(nc, x, src, dst, src_n, pay, ws, wn, bs, w_in, w1, b1, w2, b2, wf1, wf2, out):
    def sb(name, shape, dt=F32):
        return nc.alloc_sbuf_tensor(name, shape, dt)

    def pb(name, shape, dt=F32):
        return nc.alloc_psum_tensor(name, shape, dt)

    def sem(name):
        return nc.alloc_semaphore(name)

    tables = [nc.dram_tensor(f"table{i}", [N, ROW], F16).ap() for i in range(LAYERS)]
    msg_table = nc.dram_tensor("msg_table", [N, G], F32).ap()
    chunk_base = nc.dram_tensor("chunk_base", [CB * P, BINS], F32).ap()
    by_src = nc.dram_tensor("by_src", [P * CH + WIN, PAY], F32).ap()

    ident = sb("ident", [P, P])
    iota_i = sb("iota_i", [P, 640], I32)
    node_iota = sb("node_iota", [P, TN], BF16)
    node_iota32 = sb("node_iota32", [P, TN])
    tile_lo = sb("tile_lo", [P, BINS + 1])
    bias = sb("bias", [P, LAYERS, D])
    weights = sb("weights", [P, 2 * LAYERS, KC, D])
    state = sb("state", [P, TILES, D])
    inv_deg = sb("inv_deg", [P, TILES])
    meta = sb("meta", [1, TILES + 1, 4], I32)
    slots = sb("slots", [P, SLOTS, ROW], F16)
    msg_slots = slots[:, :, 0:2 * G].bitcast(F32)
    win_src = sb("win_src", [P, SLOTS], I32)
    win_dst = sb("win_dst", [P, SLOTS], I32)
    gather_idx = sb("gather_idx", [P, SLOTS], I32)
    rel = sb("rel", [P, SLOTS])
    hot = sb("hot", [P, SLOTS, TN], BF16)
    acc = sb("acc", [P, D])
    deg = sb("deg", [P, 1])
    y = sb("y", [P, D])
    h_row = sb("h_row", [P, D])
    h_t = sb("h_t", [P, KC, TN])
    row = sb("row", [P, ROW], F16)
    row_max = sb("row_max", [P, 1])
    row_pow = sb("row_pow", [P, 1], I32)
    row_inv_i = sb("row_inv_i", [P, 1], I32)
    row_inv = sb("row_inv", [P, 1])
    xt = sb("xt", [P, D])
    stats = sb("stats", [P, 6])
    mv = sb("mv", [P, 2])
    std = sb("std", [P, 1])
    rstd = sb("rstd", [P, 1])
    shift = sb("shift", [P, 1])
    msg_row = sb("msg_row", [P, G])
    arena = weights[:, 2:6, :, :].rearrange("p a k n -> p (a k n)")
    taken = [0]

    def reuse(*shape):
        n = 1
        for k in shape:
            n *= k
        part = arena[:, taken[0]:taken[0] + n]
        taken[0] += n
        assert taken[0] <= 4 * KC * D
        names = "abc"[:len(shape)]
        return part.rearrange(f"p ({' '.join(names)}) -> p {' '.join(names)}", **dict(zip(names, shape)))

    hot32 = reuse(SLOTS, TN)
    msg = reuse(2, 4 * 2 * G).rearrange("p h (j k) -> p h j k", j=4)
    m_relu = reuse(5, P)
    m_exp = reuse(5, P)
    filt_h = reuse(5, P)
    win_p = sb("win_p", [P, SLOTS, PAY])
    feat_t = reuse(5, P)
    y_cut = sb("y_cut", [P, SLOTS, YD])
    w_in_sb = sb("w_in_sb", [P, 2, F])
    w1_sb = sb("w1_sb", [4 * PAY, 4 * F])
    b1_sb = sb("b1_sb", [P, 1])
    w2_sb = sb("w2_sb", [P, 4, G])
    b2_row = sb("b2_row", [3, 4, G])
    b2_parts = sb("b2_parts", [3, 4, G], BF16)
    b2_part = sb("b2_part", [3, 3, 4 * G], BF16)
    ones3 = sb("ones3", [3, P], BF16)
    wf1_sb = sb("wf1_sb", [P, 3, B])
    wf2_sb = sb("wf2_sb", [P, 2, B])
    av = sb("av", [P, 2, 4, G])
    ab = sb("ab", [P, 4, F])
    vy = sb("vy", [P, 4, C3, F])
    vys = sb("vys", [P, 4, F])
    pairs = sb("pairs", [P, 4, 2 * F])
    pairs_t = sb("pairs_t", [P, 2, TN])
    o_relu = sb("o_relu", [P, TN])
    o_exp = sb("o_exp", [P, TN])
    o1 = sb("o1", [P, 4, TN])
    src_i = sb("src_i", [P, CH], I32)
    src_f = state[:, 22:23, 0:CH].rearrange("p a c -> p (a c)")
    base_bc = state[:, :, :].rearrange("p a k -> p (a k)")[:, 0:CH * BINS].rearrange("p (c t) -> p c t", t=BINS)
    in_bin = slots[:, :, :].rearrange("p a b -> p (a b)")[:, 0:CH * BINS].bitcast(BF16).rearrange("p (c t) -> p c t", t=BINS)
    GEC = CH // 4
    past = slots[:, :, :].rearrange("p a b -> p (a b)")[:, CH * BINS:CH * BINS + GEC * (BINS + 1)].bitcast(BF16).rearrange("p (c t) -> p c t", t=BINS + 1)
    tri = sb("tri", [P, P], BF16)
    ones = sb("ones", [P, P], BF16)
    tot = sb("tot", [P, CB, BINS], BF16)
    chunk0 = sb("chunk0", [P, CB, BINS])
    totals = sb("totals", [P, BINS])
    scan = sb("scan", [P, 2, BINS])
    start = sb("start", [P, BINS])
    place = sb("place", [P, PIECE, BINS])
    place_f = sb("place_f", [P, CH])
    place_i = sb("place_i", [P, CH], I32)
    scat_idx = sb("scat_idx", [P, 2, PIECE], I32)
    scat_row = sb("scat_row", [P, 2, PIECE, PAY])
    over_m = sb("over_m", [1, TILES, MAXR])
    row_n = sb("row_n", [1, 2, BINS])
    meta_mf = sb("meta_mf", [1, 4, TILES + 1])
    meta_m = sb("meta_m", [1, TILES + 1, 4], I32)
    dst_i = sb("dst_i", [EP, EC], I32)
    dst_f = av[0:EP, :, :, :].rearrange("p a b c -> p (a b c)")[:, 0:EC]
    bmin = sb("bmin", [P, NB])
    bmax = sb("bmax", [P, NB])
    bpos = sb("bpos", [P, NB])
    in_a = slots[0:EP, 0:9, :].rearrange("p a b -> p (a b)")[:, 0:2 * TILES * NB].bitcast(F32).rearrange("p (t b) -> p t b", t=TILES)
    in_b = slots[0:EP, 9:18, :].rearrange("p a b -> p (a b)")[:, 0:2 * TILES * NB].bitcast(F32).rearrange("p (t b) -> p t b", t=TILES)
    ends = sb("ends", [P, 2, TILES])
    ends_t = sb("ends_t", [TILES, 2])
    edge0 = sb("edge0", [TILES, 1])
    edge1 = sb("edge1", [TILES, 1])
    length = sb("length", [TILES, 1])
    steps = sb("steps", [TILES, MAXR])
    over = sb("over", [TILES, MAXR])
    rounds = sb("rounds", [TILES, 1])
    rounds1 = sb("rounds1", [TILES, 1])
    before = sb("before", [TILES, TILES + 1])
    meta_f = sb("meta_f", [1, 4, TILES + 1])

    banks = [pb(f"bank{i}", [P, D]) for i in range(8)]
    p_acc, p_t, p_n, p_s, p_deg = banks[0], banks[1], banks[2], banks[3], banks[4]
    p_mlp_a, p_mlp_b, p_o1, p_o2 = banks[2], banks[3], banks[4], banks[7]
    p_w = [banks[5], banks[6]]
    p_cnt, p_pre, p_rank = banks[5], banks[6], [banks[4], banks[7]]

    s_const = sem("consts_loaded")
    s_iota = sem("iota_made")
    s_dst = sem("dst_loaded")
    s_w0 = sem("first_weights_loaded")
    s_ends = sem("ranges_ready")
    s_meta = sem("meta_ready")
    s_set_d = sem("setup_dve")
    s_set_p = sem("setup_pe")
    s_xt = sem("x_loaded")
    s_xt_free = sem("x_used")
    s_src = sem("win_src_loaded")
    s_dstw = sem("win_dst_loaded")
    s_src_free = sem("win_src_used")
    s_dst_free = sem("win_dst_used")
    s_fw_free = sem("features_used")
    s_yw_free = sem("angles_used")
    s_ftp = sem("features_transposed")
    s_ft = sem("feat_t_ready")
    s_srcn = sem("src_loaded")
    s_bin = sem("bins_ready")
    s_cnt = sem("counted")
    s_tot = sem("tot_ready")
    s_pre = sem("counts_summed")
    s_c0 = sem("chunk0_ready")
    s_c0s = sem("chunk0_stored")
    s_bc = sem("base_loaded")
    s_tail = sem("tail_stored")
    s_rank = sem("ranked")
    s_rank_free = sem("rank_used")
    s_rank_d = sem("place_dve")
    s_place = sem("places_ready")
    s_pay = [sem("rows_loaded0"), sem("rows_loaded1")]
    s_scat = [sem("scattered0"), sem("scattered1")]
    s_sidx = sem("scat_idx_copied")
    s_idx = sem("idx_copied")
    s_g = [sem(f"gathered{j}") for j in range(SLOTS)]
    s_used = sem("slot_used")
    s_hot = sem("hot_ready")
    s_acc_free = sem("p_acc_free")
    s_y = sem("y_ready")
    s_y_free = sem("y_free")
    s_h = sem("h_ready")
    s_tp = sem("transposed")
    s_ht = sem("h_t_ready")
    s_pn = sem("pn_ready")
    s_ps = sem("ps_ready")
    s_pn_free = sem("pn_free")
    s_ps_free = sem("ps_free")
    s_inv = sem("row_scale_ready")
    s_hi = sem("row_hi_ready")
    s_row = sem("row_ready")
    s_stored = sem("row_stored")
    s_row_free = sem("row_free")
    s_deg = sem("degree_added")
    s_nd = sem("node_dve")
    s_td = sem("tile_dve")
    s_bn = sem("stats_ready")
    s_std = sem("std_ready")
    s_var = sem("var_ready")
    s_keep = sem("state_kept")
    s_mrow = sem("msg_row_ready")
    s_mstored = sem("msg_row_stored")
    s_mrow_free = sem("msg_row_free")
    s_gd = sem("group_dve")
    s_mlp = sem("mlp1_ready")
    s_mact = sem("mlp_act")
    s_mh = sem("filter_h_ready")
    s_w = sem("filters_ready")
    s_w_free = sem("filters_used")
    s_av = sem("av_ready")
    s_av2 = sem("av_scaled")
    s_m = sem("msg_ready")
    s_pairs = sem("pairs_ready")
    s_ptp = sem("pairs_transposed")
    s_pt = sem("pairs_t_ready")
    s_o1 = sem("o1_product")
    s_oact = sem("o_act")
    s_o1v = sem("o1_vectors_ready")
    s_o1s = sem("o1_scalars_ready")
    s_o2 = sem("o2_product")
    s_o2_free = sem("o2_used")
    s_out = sem("out_ready")
    s_outs = sem("out_stored")
    s_outrow_free = sem("out_row_free")


    GROUPS = [(j, min(4, SLOTS - j)) for j in range(0, SLOTS, 4)]
    NG = len(GROUPS)
    FULL = SLOTS // 4
    REST = SLOTS - 4 * FULL
    RS_B = 1.0 / float(B) ** 0.5
    RS_M = 1.0 / float(2 * F) ** 0.5
    IS3 = 1.0 / 3.0 ** 0.5

    def tile_of(buf, t, rows=TN):
        return buf[0:rows, bass.ds(t, 1), :].rearrange("p a k -> p (a k)")

    def entry(eng, k, c, lo, hi, table=meta):
        return eng.value_load(table[0:1, bass.ds(k, 1), c:c + 1].rearrange("p a k -> p (a k)"), min_val=lo, max_val=hi)

    def rounds_before(eng, ps):
        if ps == 0:
            return 0
        return entry(eng, TILES, 0, 1, TILES * MAXR) * ps

    def rounds_of(eng, t, table=meta):
        return entry(eng, t, 0, 1, TILES * MAXR, table), entry(eng, t, 1, 2, TILES * MAXR + 1, table)

    def wait_alone(eng, sem, value):
        value = eng.to_reg(value)
        eng.wait_ge(s_meta, 1)
        eng.wait_ge(sem, value)

    def msg_free(eng, r, g):
        eng.wait_ge(s_used, r * SLOTS + SLOTS + (sum(GROUPS[g - 2]) if g >= 2 else 0))

    consts = []
    blocks = []
    for l in range(LAYERS):
        consts.append((bias[:, l, :], bass.AP(bs.tensor, l * D, [[0, P], [1, D]])))
        if l:
            consts.append((weights[:, 2 * l, :, :], wn[l, :, :].rearrange("(k p) n -> p k n", p=P)))
            consts.append((weights[:, 2 * l + 1, :, :], ws[l, :, :].rearrange("(k p) n -> p k n", p=P)))
    consts.append((w_in_sb[:, :, :], w_in.rearrange("a b f -> b a f")))
    for j in range(4):
        consts.append((b1_sb[F * j:F * j + F, :], b1.rearrange("(f a) -> f a", a=1)))
        blocks.append((w2_sb[F * j:F * j + F, j, :], w2))
        blocks.append((w1_sb[PAY * j:PAY * j + R, F * j:F * j + F], w1))
        consts.append((b2_row[:, j, :], bass.AP(b2.tensor, 0, [[0, 3], [1, G]])))
    for k in range(3):
        h = 2 * F * (k % 2)
        blocks.append((wf1_sb[h:h + 2 * F, k, :], wf1[min(k, 1), :, :]))
    consts.append((wf2_sb[:, :, :], wf2.rearrange("a b d -> b a d")))
    ALL_CONSTS = 16 * (len(consts) + len(blocks))

    with nc.Block() as block:

        @block.sync
        def _(sp):
            sp.sem_inc(s_row_free, 1)
            sp.sem_inc(s_mrow_free, 1)
            sp.sem_inc(s_outrow_free, 1)
            sp.dma_start(dst_i[:, :], dst[0:E].rearrange("(p c) -> p c", p=EP)).then_inc(s_dst, 16)

            def load_x(t):
                sp.wait_ge(s_y_free, t + 1)
                sp.dma_start(y[0:TN, :], x[bass.ds(t * TN, TN), :]).then_inc(s_xt, 16)

            def store_row(i, ps, t):
                sp.wait_ge(s_row, i)
                sp.dma_start(tables[ps][bass.ds(t * TN, TN), :], row[0:TN, :]).then_inc(s_stored, 16)
                wait_alone(sp, s_stored, i * 16)
                sp.sem_inc(s_row_free, 1)

            sp.dma_start(src_i[:, :], src_n.rearrange("(p c) -> p c", p=P)).then_inc(s_srcn, 16)
            sp.dma_start(by_src[P * CH:P * CH + WIN, :], pay[E:E + WIN, :]).then_inc(s_tail, 16)
            load_x(0)
            sp.dma_start(weights[:, 0, :, :], wn[0, :, :].rearrange("(k p) n -> p k n", p=P)).then_inc(s_w0, 16)
            sp.dma_start(weights[:, 1, :, :], ws[0, :, :].rearrange("(k p) n -> p k n", p=P)).then_inc(s_w0, 16)
            for to, of in consts:
                sp.dma_start(to, of).then_inc(s_const, 16)
            sp.wait_ge(s_iota, 10)
            for to, of in blocks:
                sp.dma_start(to, of).then_inc(s_const, 16)
            rows = pay[0:P * CH, :].rearrange("(p c) k -> p c k", p=P)

            def load_rows(k, half):
                sp.dma_start(scat_row[:, half, :, :], rows[:, bass.ds(k * PIECE, PIECE), :]).then_inc(s_pay[half], 16)

            load_rows(0, 0)
            load_rows(1, 1)
            sp.wait_ge(s_c0, 1)
            sp.dma_start(chunk_base.rearrange("(b p) t -> p b t", p=P), chunk0[:, :, :]).then_inc(s_c0s, 16)
            sp.wait_ge(s_c0s, 16)
            sp.dma_start(base_bc.rearrange("p c t -> p (c t)"), bass.AP(chunk_base.tensor, 0, [[0, P], [1, CH * BINS]])).then_inc(s_bc, 16)
            with sp.Fori(0, (TILES - 1) // 2) as u:
                for half in range(2):
                    load_x(u * 2 + half + 1)
                    store_row(u * 2 + half + 1, 0, u * 2 + half)
                    sp.wait_ge(s_scat[half], u * (16 * PIECE) + 16 * PIECE)
                    load_rows(u * 2 + half + 2, half)
            store_row(TILES, 0, TILES - 1)

            sp.wait_ge(s_meta, 1)

            def load_windows(ps, t, base):
                table = meta_m if ps == LAYERS else meta
                q0, q1 = rounds_of(sp, t, table)
                e0 = entry(sp, t, 2, 0, E, table)
                with sp.Fori(q0, q1) as q:
                    r = q + base
                    e = nc.s_assert_within(e0 + (q - q0) * WIN, 0, E,
                                           skip_runtime_bounds_check_because="a tile's rounds start inside its range of the list")
                    sp.wait_ge(s_src_free, r)
                    if ps < LAYERS:
                        sp.dma_start(win_src[:, :], src[bass.ds(e, WIN)].rearrange("(p j) -> p j", j=SLOTS)).then_inc(s_src, 16)
                    sp.wait_ge(s_dst_free, r)
                    if ps < LAYERS:
                        sp.dma_start(win_dst[:, :], dst[bass.ds(e, WIN)].rearrange("(p j) -> p j", j=SLOTS)).then_inc(s_dstw, 16)
                    else:
                        wait_alone(sp, s_yw_free, q)
                        wait_alone(sp, s_fw_free, q)
                        sp.dma_start(win_p[:, :, :], by_src[bass.ds(e, WIN), :].rearrange("(p j) k -> p j k", j=SLOTS)).then_inc(s_src, 16)

            for ps in range(LAYERS - 1):
                base = rounds_before(sp, ps)
                load_windows(ps, 0, base)
                load_windows(ps, 1, base)
                with sp.Fori(1, TILES - 1) as t:
                    load_windows(ps, t + 1, base)
                    store_row((ps + 1) * TILES + t, ps + 1, t - 1)
                store_row((ps + 2) * TILES - 1, ps + 1, TILES - 2)
                store_row((ps + 2) * TILES, ps + 1, TILES - 1)

            def load_res(t):
                sp.wait_ge(s_xt_free, t + 1)
                sp.dma_start(xt[0:TN, :], x[bass.ds(t * TN, TN), :]).then_inc(s_xt, 16)

            def store_msg(t):
                sp.wait_ge(s_mrow, t + 1)
                sp.dma_start(msg_table[bass.ds(t * TN, TN), :], msg_row[0:TN, :]).then_inc(s_mstored, 16)
                sp.wait_ge(s_mstored, (t + 1) * 16)
                sp.sem_inc(s_mrow_free, 1)

            base = rounds_before(sp, LAYERS - 1)
            load_windows(LAYERS - 1, 0, base)
            load_res(0)
            load_windows(LAYERS - 1, 1, base)
            with sp.Fori(1, TILES - 1) as t:
                load_windows(LAYERS - 1, t + 1, base)
                load_res(t)
                store_msg(t - 1)
            load_res(TILES - 1)
            store_msg(TILES - 2)
            store_msg(TILES - 1)

            def store_out(t):
                sp.wait_ge(s_out, t + 1)
                sp.dma_start(out[bass.ds(t * TN, TN), :], h_row[0:TN, :]).then_inc(s_outs, 16)
                sp.wait_ge(s_outs, (t + 1) * 16)
                sp.sem_inc(s_outrow_free, 1)

            base = rounds_before(sp, LAYERS)
            for half in range(2):
                sp.wait_ge(s_scat[half], 16 * PIECE * PIECES // 2)
            sp.wait_ge(s_tail, 16)
            load_windows(LAYERS, 0, base)
            load_windows(LAYERS, 1, base)
            with sp.Fori(1, TILES - 1) as t:
                load_windows(LAYERS, t + 1, base)
                store_out(t - 1)
            total = entry(sp, TILES, 0, 1, TILES * MAXR, meta_m)
            wait_alone(sp, s_src_free, total + base + 1)
            wait_alone(sp, s_dst_free, total + base + 1)
            wait_alone(sp, s_yw_free, total + 1)
            wait_alone(sp, s_fw_free, total + 1)
            sp.dma_start(win_p[:, :, :], by_src[0:WIN, :].rearrange("(p j) k -> p j k", j=SLOTS)).then_inc(s_src, 16)
            store_out(TILES - 2)
            store_out(TILES - 1)

        @block.gpsimd
        def _(pool):
            pool.sem_inc(s_src_free, 1)
            pool.sem_inc(s_idx, 2)
            pool.iota(iota_i[:, 0:TN], [[1, TN]], base=0, channel_multiplier=0).then_inc(s_iota, 1)
            pool.iota(iota_i[:, 128:128 + BINS + 1], [[TN, BINS + 1]], base=0, channel_multiplier=0).then_inc(s_iota, 1)
            pool.iota(iota_i[:, 160:160 + NB], [[BLK, NB]], base=0, channel_multiplier=EC).then_inc(s_iota, 1)
            pool.iota(iota_i[:, 256:256 + MAXR], [[WIN, MAXR]], base=WIN, channel_multiplier=0).then_inc(s_iota, 1)
            pool.iota(iota_i[:, 300:300 + TILES + 1], [[1, TILES + 1]], base=0, channel_multiplier=-1).then_inc(s_iota, 1)
            pool.memset(ident[:, :], 0.0).then_inc(s_iota, 1)
            pool.wait_ge(s_iota, 6)
            pool.affine_select(out=ident[:, :], in_=ident[:, :], compare_op=ALU.not_equal, fill=1.0,
                               base=0, pattern=[[-1, P]], channel_multiplier=1).then_inc(s_iota, 1)
            pool.memset(w2_sb[:, :, :], 0.0).then_inc(s_iota, 1)
            pool.memset(wf1_sb[:, :, :], 0.0).then_inc(s_iota, 1)
            pool.memset(w1_sb[:, :], 0.0).then_inc(s_iota, 1)
            pool.iota(iota_i[:, 500:500 + P], [[1, P]], base=0, channel_multiplier=-1).then_inc(s_iota, 1)
            pool.wait_ge(s_meta, 1)

            pool.wait_ge(s_tail, 16)

            def scatter(u, half, count):
                k = u * 2 + half
                pool.wait_ge(s_place, k + 1)
                pool.wait_ge(s_pay[half], count)
                pool.wait_ge(s_iota, 11)
                pool.tensor_copy(scat_idx[:, half, :], place_i[:, bass.ds(k * PIECE, PIECE)]).then_inc(s_sidx, 1)
                wait_alone(pool, s_sidx, k + 1)
                for j in range(PIECE):
                    pool.indirect_dma_start(
                        out=by_src[0:P * CH, :], out_offset=bass.IndirectOffsetOnAxis(ap=scat_idx[:, half, j:j + 1], axis=0),
                        in_=scat_row[:, half, j, :], in_offset=None).then_inc(s_scat[half], 16)

            with pool.Fori(0, PIECES // 2) as u:
                for half in range(2):
                    scatter(u, half, u * 16 + 16)

            for ps in range(PASSES):
                base = rounds_before(pool, ps)
                if ps < LAYERS:
                    pool.wait_ge(s_stored, 16 * TILES * (ps + 1))
                else:
                    pool.wait_ge(s_mstored, 16 * TILES)
                with pool.Fori(0, TILES) as t:
                    q0, q1 = rounds_of(pool, t, meta_m if ps == LAYERS else meta)
                    with pool.Fori(q0, q1) as q:
                        r = q + base
                        pool.wait_ge(s_src, r * 16)
                        for j in range(SLOTS):
                            if j % HALF == 0:
                                wait_alone(pool, s_used, r * SLOTS + j + HALF)
                                of = win_p[:, j:j + HALF, PAY_DST].bitcast(I32) if ps == LAYERS else win_src[:, j:j + HALF]
                                pool.tensor_copy(gather_idx[:, j:j + HALF], of).then_inc(s_idx, 1)
                                pool.wait_ge(s_idx, r * 2 + 1 + j // HALF)
                                if j:
                                    pool.sem_inc(s_src_free, 1)
                            wait_alone(pool, s_used, r * SLOTS + j + 1)
                            if ps < LAYERS:
                                to, table = slots[:, j, :], tables[ps]
                            else:
                                to, table = slots[:, j, 0:2 * G].bitcast(F32), msg_table
                            pool.indirect_dma_start(
                                out=to, out_offset=None, in_=table[:, :],
                                in_offset=bass.IndirectOffsetOnAxis(ap=gather_idx[:, j:j + 1], axis=0),
                            ).then_inc(s_g[j], 16)

        @block.tensor
        def _(pe):
            pe.sem_inc(s_used, 2 * SLOTS)
            pe.sem_inc(s_fw_free, 1)
            for s in (s_tp, s_pn, s_ps, s_ptp, s_o1, s_o2, s_ftp, s_mlp):
                pe.sem_inc(s, 1)
            pe.sem_inc(s_w, NG)
            pe.wait_ge(s_iota, 7)
            pe.wait_ge(s_ends, 1)
            for k in range(2):
                last = pe.transpose(p_t[0:TILES, k * P:k * P + EP], ends[0:EP, k, :], ident[0:EP, 0:EP])
            last.then_inc(s_set_p, 1)
            pe.wait_ge(s_ends, 2)
            pe.matmul(p_n[0:1, 0:TILES + 1], rounds[:, :], before[:, :], start=True, stop=True)
            pe.matmul(p_n[0:1, 32:32 + TILES], rounds[:, :], ident[0:TILES, 0:TILES], start=True, stop=True)
            pe.matmul(p_n[0:1, 64:64 + TILES], edge0[:, :], ident[0:TILES, 0:TILES], start=True, stop=True).then_inc(s_set_p, 1)
            pe.wait_ge(s_bin, 1)
            for b in range(CB):
                n = min(P, CH - b * P)
                for k in range(BINS):
                    last = pe.matmul(p_cnt[0:n, b * BINS + k:b * BINS + k + 1], in_bin[:, b * P:b * P + n, k], ones[:, 0:1], start=True, stop=True)
            last.then_inc(s_cnt, 1)
            pe.wait_ge(s_tot, 1)
            for b in range(CB):
                for a in range(b):
                    pe.matmul(p_pre[:, b * BINS:(b + 1) * BINS], ones[:, :], tot[:, a, :], start=a == 0, stop=False)
                pe.matmul(p_pre[:, b * BINS:(b + 1) * BINS], tri[:, :], tot[:, b, :], start=b == 0, stop=True)
            for a in range(CB):
                last = pe.matmul(p_pre[:, 256:256 + BINS], ones[:, :], tot[:, a, :], start=a == 0, stop=a == CB - 1)
            last.then_inc(s_pre, 1)
            with pe.Fori(0, PIECES // 2) as u:
                for half in range(2):
                    k = u * 2 + half
                    pe.wait_ge(s_rank_free, k + 1)
                    pe.matmul(p_rank[half][:, 0:PIECE * BINS], tri[:, :],
                              in_bin[:, bass.ds(k * PIECE, PIECE), :].rearrange("p c t -> p (c t)"), start=True, stop=True).then_inc(s_rank, 1)
            pe.wait_ge(s_meta, 1)

            def node(i, l):
                pe.wait_ge(s_h, i)
                pe.wait_ge(s_ht, i)
                for k in range(KC):
                    last = pe.transpose(p_t[:, k * P:k * P + TN], h_row[0:TN, k * P:(k + 1) * P], ident[0:TN, 0:TN])
                last.then_inc(s_tp, 1)
                pe.wait_ge(s_ht, i + 1)
                pe.wait_ge(s_pn_free, i)
                for k in range(KC):
                    last = pe.matmul(p_n[0:TN, :], h_t[:, k, :], weights[:, 2 * l, k, :], start=k == 0, stop=k == KC - 1)
                last.then_inc(s_pn, 1)
                pe.wait_ge(s_ps_free, i)
                for k in range(KC):
                    last = pe.matmul(p_s[0:TN, :], h_t[:, k, :], weights[:, 2 * l + 1, k, :], start=k == 0, stop=k == KC - 1)
                last.then_inc(s_ps, 1)

            def aggregate(ps, t, base):
                q0, q1 = rounds_of(pe, t)
                with pe.Fori(q0, q1) as q:
                    r = q + base
                    pe.wait_ge(s_acc_free, r)
                    for j in range(SLOTS):
                        pe.wait_ge(s_hot, r * SLOTS + j + 1)
                        first, end = j == 0, j == SLOTS - 1
                        if ps == 0:
                            pe.matmul(p_deg[0:TN, 0:1], hot[:, j, :], slots[:, j, ISC:ISC + 1].bitcast(BF16), start=first, stop=end)
                        pe.matmul(p_acc[0:TN, :], hot[:, j, :], slots[:, j, HI:HI + D], start=first, stop=False)
                        pe.matmul(p_acc[0:TN, :], hot[:, j, :], slots[:, j, LO:LO + D], start=False, stop=end).then_inc(s_used, 1)

            pe.wait_ge(s_w0, 32)
            with pe.Fori(0, TILES) as t:
                node(t + 1, 0)
            pe.wait_ge(s_const, ALL_CONSTS)
            for ps in range(LAYERS - 1):
                base = rounds_before(pe, ps)
                aggregate(ps, 0, base)
                with pe.Fori(1, TILES) as t:
                    aggregate(ps, t, base)
                    node((ps + 1) * TILES + t, ps + 1)
                node((ps + 2) * TILES, ps + 1)

            def msg_node(t):
                i = LAYERS * TILES + t + 1
                pe.wait_ge(s_h, i)
                pe.wait_ge(s_ht, i)
                for k in range(4):
                    cols = h_row[0:TN, 0:B] if k == 0 else h_row[0:TN, B:4 * B].rearrange("p (b c) -> p c b", c=C3)[:, k - 1, :]
                    last = pe.transpose(p_t[:, k * P:k * P + TN], cols, ident[0:TN, 0:TN])
                last.then_inc(s_tp, 1)
                pe.wait_ge(s_ht, i + 1)
                pe.wait_ge(s_pn_free, i)
                for k in range(4):
                    last = pe.matmul(p_n[0:TN, k * F:(k + 1) * F], h_t[:, k, :], w_in_sb[:, min(k, 1), :], start=True, stop=True)
                last.then_inc(s_pn, 1)

            base = rounds_before(pe, LAYERS - 1)
            aggregate(LAYERS - 1, 0, base)
            with pe.Fori(1, TILES) as t:
                aggregate(LAYERS - 1, t, base)
                msg_node(t - 1)
            msg_node(TILES - 1)
            pe.wait_ge(s_pn_free, (LAYERS + 1) * TILES + 1)

            def features(q, r):
                wait_alone(pe, s_src, r * 16)
                wait_alone(pe, s_mact, q * 6)
                for g, (j0, n) in enumerate(GROUPS):
                    o = p_t[0:n * PAY, g * P:(g + 1) * P] if g < FULL else p_mlp_b[0:n * PAY, P:2 * P]
                    last = pe.transpose(o, win_p[:, j0:j0 + n, :].rearrange("p j k -> p (j k)"), ident[:, :])
                last.then_inc(s_ftp, 1)
                pe.wait_ge(s_ftp, q + 1)
                pe.sem_inc(s_fw_free, 1)

            def hidden(q):
                pe.wait_ge(s_ft, q)
                pe.wait_ge(s_mact, q * 6)
                for g, (j0, n) in enumerate(GROUPS):
                    o = p_mlp_a[0:n * F, g * P:(g + 1) * P] if g < FULL else p_mlp_b[0:n * F, 0:P]
                    last = pe.matmul(o, w1_sb[0:n * PAY, 0:n * F], feat_t[0:n * PAY, g, :], start=True, stop=True)
                last.then_inc(s_mlp, 1)

            def filters(q, g):
                j0, n = GROUPS[g]
                pe.wait_ge(s_w_free, q * NG + max(g - 1, 0))
                w = p_w[g % 2]
                pe.matmul(w[:, 0:n * G], ones3[:, :], b2_parts[:, 0:n, :].rearrange("k a b -> k (a b)"),
                          start=True, stop=False)
                pe.matmul(w[:, 0:n * G], filt_h[0:n * F, g, :], w2_sb[0:n * F, 0:n, :].rearrange("k a b -> k (a b)"),
                          start=False, stop=True).then_inc(s_w, 1)

            def messages(t, base):
                q0, q1 = rounds_of(pe, t, meta_m)
                with pe.Fori(q0, q1) as q:
                    r = q + base
                    pe.wait_ge(s_mh, q + 1)
                    filters(q, 0)
                    pe.wait_ge(s_acc_free, r)
                    for g, (j0, n) in enumerate(GROUPS):
                        if g + 1 < NG:
                            filters(q, g + 1)
                        if g + 3 == NG:
                            features(q + 1, r + 1)
                        if g + 2 == NG:
                            hidden(q + 1)
                        pe.wait_ge(s_m, q * NG + g + 1)
                        pe.wait_ge(s_av2, q * NG + g + 1)
                        for j in range(n):
                            pe.matmul(p_acc[0:TN, 0:2 * G], hot32[:, j0 + j, :], msg[:, g % 2, j, :],
                                      start=j0 + j == 0, stop=j0 + j == SLOTS - 1).then_inc(s_used, 1)

            def output(t):
                pe.wait_ge(s_pairs, t + 1)
                pe.wait_ge(s_pt, t + 1)
                for k in range(2):
                    last = pe.transpose(p_t[:, k * P:k * P + TN], pairs[0:TN, 2 * k:2 * k + 2, :].rearrange("p a b -> p (a b)"), ident[0:TN, 0:TN])
                last.then_inc(s_ptp, 1)
                pe.wait_ge(s_pt, t + 2)
                pe.wait_ge(s_o1v, t + 1)
                for k, w in enumerate((0, 1, 2, 1)):
                    last = pe.matmul(p_o1[:, k * P:k * P + TN], wf1_sb[:, w, :], pairs_t[:, k // 2, :], start=True, stop=True)
                last.then_inc(s_o1, 1)
                pe.wait_ge(s_o1v, t + 2)
                pe.wait_ge(s_o1s, t + 2)
                pe.wait_ge(s_o2_free, t + 1)
                for k in range(4):
                    last = pe.matmul(p_o2[0:TN, k * P:(k + 1) * P], o1[:, k, :], wf2_sb[:, min(k, 1), :], start=True, stop=True)
                last.then_inc(s_o2, 1)

            base = rounds_before(pe, LAYERS)
            features(1, base + 1)
            hidden(1)
            messages(0, base)
            with pe.Fori(1, TILES) as t:
                messages(t, base)
                output(t - 1)
            output(TILES - 1)

        @block.scalar
        def _(act):
            for s in (s_y_free, s_ht, s_keep, s_pt, s_o1v):
                act.sem_inc(s, 1)
            act.sem_inc(s_mact, 6)
            act.sem_inc(s_av2, NG)

            def transposed(i):
                act.wait_ge(s_tp, i + 1)
                act.wait_ge(s_pn, i)
                act.activation(h_t[:, :, :], p_t[:, :].rearrange("p (k n) -> p k n", k=KC)[:, :, 0:TN], ACT.Copy).then_inc(s_ht, 1)

            def node(i):
                act.wait_ge(s_ps, i)
                transposed(i)
                act.wait_ge(s_inv, i)
                act.wait_ge(s_row_free, i)
                act.activation(row[0:TN, HI:HI + D], p_n[0:TN, :], ACT.Copy, scale=row_inv[0:TN, 0:1]).then_inc(s_hi, 1)

            def rows_in(i, func):
                act.wait_ge(s_tp, i)
                act.activation(h_row[0:TN, :], y[0:TN, :], func).then_inc(s_h, 1)
                act.wait_ge(s_h, i)
                act.sem_inc(s_y_free, 1)

            with act.Fori(0, TILES) as t:
                act.wait_ge(s_xt, t * 16 + 16)
                rows_in(t + 1, ACT.Copy)
                node(t + 1)
            for ps in range(LAYERS - 1):
                i0 = (ps + 1) * TILES
                act.wait_ge(s_y, ps * TILES + 1)
                rows_in(i0 + 1, ACT.Relu)
                with act.Fori(1, TILES) as t:
                    node(t + i0)
                    act.wait_ge(s_y, t + ps * TILES + 1)
                    rows_in(t + i0 + 1, ACT.Relu)
                node(i0 + TILES)
            act.wait_ge(s_ps, LAYERS * TILES + 1)

            def root(k):
                act.wait_ge(s_var, k)
                act.activation(std[0:TN, :], mv[0:TN, 1:2], ACT.Sqrt).then_inc(s_std, 1)

            def keep(t):
                act.wait_ge(s_h, t + LAYERS * TILES + 1)
                act.activation(tile_of(state, t), h_row[0:TN, :], ACT.Copy).then_inc(s_keep, 1)

            def msg_node(t):
                i = t + LAYERS * TILES + 1
                transposed(i)
                act.wait_ge(s_pn, i + 1)
                act.wait_ge(s_mrow_free, t + 1)
                act.activation(msg_row[0:TN, :], p_n[0:TN, 0:G], ACT.Copy, scale=RS_B).then_inc(s_mrow, 1)
                act.wait_ge(s_mrow, t + 1)
                act.sem_inc(s_pn_free, 1)

            root(1)
            keep(0)
            with act.Fori(1, TILES) as t:
                msg_node(t - 1)
                root(t + 1)
                keep(t)
            msg_node(TILES - 1)

            def hidden(q):
                act.wait_ge(s_mlp, q + 1)
                act.wait_ge(s_mh, q)
                rows = F * REST
                parts = [(p_mlp_a[:, :], slice(0, P), slice(0, FULL)), (p_mlp_b[0:rows, 0:P], slice(0, rows), slice(FULL, FULL + 1))]
                parts = [(a, b, c) for a, b, c in parts if b.stop]
                for a, b, c in parts:
                    act.activation(m_relu[b, c, :].rearrange("p g e -> p (g e)"), a, ACT.Relu, bias=b1_sb[b, :])
                for a, b, c in parts:
                    act.activation(m_exp[b, c, :].rearrange("p g e -> p (g e)"), a, ACT.Abs, bias=b1_sb[b, :]).then_inc(s_mact, 1)
                act.wait_ge(s_mact, q * 6 + 2)
                for _, b, c in parts:
                    act.activation(m_exp[b, c, :], m_exp[b, c, :], ACT.Exp, scale=-1.0).then_inc(s_mact, 1)
                act.wait_ge(s_mact, q * 6 + 4)
                for _, b, c in parts:
                    act.activation(m_exp[b, c, :], m_exp[b, c, :], ACT.Ln, bias=1.0).then_inc(s_mact, 1)

            def features(q):
                act.wait_ge(s_ftp, q + 1)
                act.wait_ge(s_mlp, q)
                act.activation(feat_t[0:4 * PAY, 0:FULL, :], p_t[0:4 * PAY, 0:FULL * P].rearrange("p (g e) -> p g e", g=FULL), ACT.Copy)
                last = act.activation(feat_t[0:REST * PAY, FULL, :], p_mlp_b[0:REST * PAY, P:2 * P], ACT.Copy)
                last.then_inc(s_ft, 1)

            def scaled(q, r, g):
                j0, n = GROUPS[g]
                act.wait_ge(s_av, q * NG + g + 1)
                msg_free(act, r, g)
                for j in range(n):
                    last = act.activation(msg[:, g % 2, j, 0:G], av[:, g % 2, j, :], ACT.Copy, scale=y_cut[:, j0 + j, 0:1])
                last.then_inc(s_av2, 1)

            def messages(t, base):
                q0, q1 = rounds_of(act, t, meta_m)
                with act.Fori(q0, q1) as q:
                    r = q + base
                    for g in range(NG):
                        if g + 2 == NG:
                            features(q + 1)
                        if g + 1 == NG:
                            hidden(q + 1)
                        scaled(q, r, g)

            def output(t):
                act.wait_ge(s_ptp, t + 2)
                act.wait_ge(s_o1, t + 1)
                act.activation(pairs_t[:, :, :], p_t[:, 0:2 * P].rearrange("p (k n) -> p k n", k=2)[:, :, 0:TN], ACT.Copy).then_inc(s_pt, 1)
                act.wait_ge(s_o1, t + 2)
                act.wait_ge(s_o1s, t + 1)
                act.activation(o_relu[:, :], p_o1[:, 0:TN], ACT.Relu, scale=RS_M)
                act.activation(o_exp[:, :], p_o1[:, 0:TN], ACT.Abs, scale=RS_M).then_inc(s_oact, 1)
                act.wait_ge(s_o2, t + 1)
                act.activation(o1[:, 1:4, :], p_o1[:, P:4 * P].rearrange("p (k n) -> p k n", k=3)[:, :, 0:TN], ACT.Copy, scale=RS_M).then_inc(s_o1v, 1)
                act.wait_ge(s_oact, t * 3 + 1)
                act.activation(o_exp[:, :], o_exp[:, :], ACT.Exp, scale=-1.0).then_inc(s_oact, 1)
                act.wait_ge(s_oact, t * 3 + 2)
                act.activation(o_exp[:, :], o_exp[:, :], ACT.Ln, bias=1.0).then_inc(s_oact, 1)
                root(t + TILES + 1)

            base = rounds_before(act, LAYERS)
            features(1)
            hidden(1)
            messages(0, base)
            with act.Fori(1, TILES) as t:
                messages(t, base)
                output(t - 1)
            output(TILES - 1)

        @block.vector
        def _(dve):
            for s in (s_dst_free, s_acc_free, s_pn_free, s_ps_free, s_xt_free, s_yw_free, s_mh, s_o1s, s_o2_free):
                dve.sem_inc(s, 1)
            dve.sem_inc(s_hot, SLOTS)
            for s in (s_w_free, s_av, s_m):
                dve.sem_inc(s, NG)
            dve.sem_inc(s_rank_free, 2)
            dve.sem_inc(s_rank_d, 1)
            dve.sem_inc(s_gd, 3 * NG)
            ch = Chain(dve, s_set_d)
            dve.wait_ge(s_iota, 11)
            dve.tensor_copy(node_iota[:, :], iota_i[:, 0:TN])
            dve.tensor_copy(node_iota32[:, :], iota_i[:, 0:TN])
            dve.tensor_copy(tile_lo[:, :], iota_i[:, 128:128 + BINS + 1])
            dve.tensor_scalar(tri[:, :], iota_i[:, 500:500 + P], 0.0, None, ALU.is_gt)
            dve.memset(ones[:, :], 1.0)
            dve.memset(tot[:, :, :], 0.0)
            dve.tensor_copy(bpos[:, :], iota_i[:, 160:160 + NB])
            dve.tensor_copy(steps[:, :], iota_i[0:TILES, 256:256 + MAXR])
            ch.link(dve.tensor_scalar(before[:, :], iota_i[0:TILES, 300:300 + TILES + 1], 0.0, None, ALU.is_gt))
            dve.wait_ge(s_dst, 16)
            ch.link(dve.tensor_copy(dst_f, dst_i[:, :]))
            blocks = dst_f.rearrange("p (b e) -> p b e", e=BLK)
            dve.tensor_reduce(bmin[0:EP, :], blocks, AX.X, ALU.min)
            ch.link(dve.tensor_reduce(bmax[0:EP, :], blocks, AX.X, ALU.max))
            lo = tile_lo[0:EP, 0:TILES].unsqueeze(2).broadcast_to([EP, TILES, NB])
            pos = bpos[0:EP, :].unsqueeze(1).broadcast_to([EP, TILES, NB])
            ch.link(dve.tensor_tensor(in_a, bmax[0:EP, :].unsqueeze(1).broadcast_to([EP, TILES, NB]), lo, ALU.is_ge))
            ch.link(dve.tensor_scalar(bmin[0:EP, :], bmin[0:EP, :], float(TN - 1), None, ALU.subtract))
            ch.link(dve.tensor_tensor(in_b, bmin[0:EP, :].unsqueeze(1).broadcast_to([EP, TILES, NB]), lo, ALU.is_le))
            ch.link(dve.tensor_tensor(in_a, in_a, in_b, ALU.mult))
            ch.link(dve.tensor_scalar(in_a, in_a, BIG, None, ALU.mult))
            ch.link(dve.tensor_tensor(in_b, pos, in_a, ALU.subtract))
            dve.tensor_reduce(ends[0:EP, 0, :], in_b, AX.X, ALU.min)
            ch.link(dve.tensor_tensor(in_a, pos, in_a, ALU.add))
            dve.tensor_reduce(ends[0:EP, 1, :], in_a, AX.X, ALU.max).then_inc(s_ends, 1)
            dve.wait_ge(s_set_p, 1)
            dve.tensor_reduce(edge0[:, :], p_t[0:TILES, 0:EP], AX.X, ALU.min)
            ch.link(dve.tensor_reduce(edge1[:, :], p_t[0:TILES, P:P + EP], AX.X, ALU.max))
            ch.link(dve.tensor_scalar(edge0[:, :], edge0[:, :], BIG, float(E), ALU.add, ALU.min))
            ch.link(dve.tensor_scalar(edge1[:, :], edge1[:, :], BIG - BLK, None, ALU.subtract))
            ch.link(dve.tensor_tensor(length[:, :], edge1[:, :], edge0[:, :], ALU.subtract))
            ch.link(dve.tensor_scalar(over[:, :], steps[:, :], length[:, 0:1], None, ALU.is_lt))
            ch.link(dve.tensor_reduce(rounds[:, :], over[:, :], AX.X, ALU.add))
            ch.link(dve.tensor_scalar(rounds[:, :], rounds[:, :], 1.0, None, ALU.add))
            dve.sem_inc(s_ends, 1)
            dve.wait_ge(s_set_p, 2)
            dve.tensor_copy(meta_f[:, 2, 0:TILES], p_n[0:1, 64:64 + TILES])
            dve.tensor_copy(meta_f[:, 3, 0:TILES], p_n[0:1, 32:32 + TILES])
            ch.link(dve.tensor_scalar(meta_f[:, 0, :], p_n[0:1, 0:TILES + 1], 1.0, None, ALU.add))
            ch.link(dve.tensor_tensor(meta_f[:, 1, 0:TILES], meta_f[:, 0, 0:TILES], meta_f[:, 3, 0:TILES], ALU.add))
            ch.link(dve.tensor_copy(meta[:, 0:TILES, 0:3], meta_f[:, 0:3, 0:TILES].rearrange("p a t -> p t a")))
            ch.link(dve.tensor_copy(meta[:, TILES, 0:1], p_n[0:1, TILES:TILES + 1]))

            dve.wait_ge(s_srcn, 16)
            ch.link(dve.tensor_copy(src_f, src_i[:, :]))
            for c in range(0, CH, GEC):
                ch.link(dve.tensor_tensor(past, src_f[:, c:c + GEC].unsqueeze(2).broadcast_to([P, GEC, BINS + 1]),
                                          tile_lo[:, :].unsqueeze(1).broadcast_to([P, GEC, BINS + 1]), ALU.is_ge))
                ch.link(dve.tensor_tensor(in_bin[:, c:c + GEC, :], past[:, :, 0:BINS], past[:, :, 1:BINS + 1], ALU.subtract))
            dve.sem_inc(s_bin, 1)
            dve.wait_ge(s_cnt, 1)
            for b in range(CB):
                n = min(P, CH - b * P)
                last = dve.tensor_copy(tot[0:n, b, :], p_cnt[0:n, b * BINS:(b + 1) * BINS])
            last.then_inc(s_tot, 1)
            dve.wait_ge(s_pre, 1)
            ch.link(dve.tensor_copy(totals[:, :], p_pre[:, 256:256 + BINS]))

            def prefix(bufs, of, n, end):
                ch.link(dve.tensor_copy(bufs[0], of))
                d, k = 1, 0
                while d < n:
                    dve.tensor_copy(bufs[1 - k][:, 0:d], bufs[k][:, 0:d])
                    ch.link(dve.tensor_tensor(bufs[1 - k][:, d:n], bufs[k][:, d:n], bufs[k][:, 0:n - d], ALU.add))
                    d, k = 2 * d, 1 - k
                ch.link(dve.tensor_tensor(end, bufs[k], of, ALU.subtract))

            prefix([scan[:, 0, :], scan[:, 1, :]], totals[:, :], BINS, start[:, :])
            dve.tensor_tensor(chunk0[:, :, :], p_pre[:, 0:CB * BINS].rearrange("p (b t) -> p b t", b=CB),
                              start[:, :].unsqueeze(1).broadcast_to([P, CB, BINS]), ALU.add).then_inc(s_c0, 1)
            ch.link(dve.tensor_tensor(over_m[:, :, :], totals[0:1, 0:TILES].unsqueeze(2).broadcast_to([1, TILES, MAXR]),
                                      steps[0:1, :].unsqueeze(1).broadcast_to([1, TILES, MAXR]), ALU.is_gt))
            ch.link(dve.memset(meta_mf[:, :, :], 0.0))
            ch.link(dve.tensor_reduce(meta_mf[:, 3, 0:TILES], over_m[:, :, :], AX.X, ALU.add))
            ch.link(dve.tensor_scalar(meta_mf[:, 3, 0:TILES], meta_mf[:, 3, 0:TILES], 1.0, None, ALU.add))
            prefix([row_n[:, 0, :], row_n[:, 1, :]], meta_mf[:, 3, :], TILES + 1, meta_mf[:, 0, :])
            ch.link(dve.tensor_copy(meta_m[:, TILES, 0:1], meta_mf[:, 0, TILES:TILES + 1]))
            ch.link(dve.tensor_scalar(meta_mf[:, 0, :], meta_mf[:, 0, :], 1.0, None, ALU.add))
            ch.link(dve.tensor_tensor(meta_mf[:, 1, 0:TILES], meta_mf[:, 0, 0:TILES], meta_mf[:, 3, 0:TILES], ALU.add))
            ch.link(dve.tensor_copy(meta_mf[:, 2, 0:TILES], start[0:1, 0:TILES]))
            ch.link(dve.tensor_copy(meta_m[:, 0:TILES, 0:3], meta_mf[:, 0:3, 0:TILES].rearrange("p a t -> p t a")))
            dve.sem_inc(s_meta, 1)

            dve.wait_ge(s_bc, 16)
            with dve.Fori(0, PIECES // 2) as u:
                for half in range(2):
                    k = u * 2 + half
                    part = bass.ds(k * PIECE, PIECE)
                    dve.wait_ge(s_rank, k + 1)
                    dve.tensor_tensor(place[:, :, :], p_rank[half][:, 0:PIECE * BINS].rearrange("p (c t) -> p c t", t=BINS),
                                      base_bc[:, part, :], ALU.add).then_inc(s_rank_free, 1)
                    dve.wait_ge(s_rank_free, k + 3)
                    dve.tensor_tensor(place[:, :, :], place[:, :, :], in_bin[:, part, :], ALU.mult).then_inc(s_rank_d, 1)
                    dve.wait_ge(s_rank_d, k * 2 + 2)
                    dve.tensor_reduce(place_f[:, part], place[:, :, :], AX.X, ALU.add).then_inc(s_rank_d, 1)
                    dve.wait_ge(s_rank_d, k * 2 + 3)
                    dve.tensor_copy(place_i[:, part], place_f[:, part]).then_inc(s_place, 1)

            def node(i, l, t):
                ch = Chain(dve, s_nd, (i - 1) * NODE_STEPS)
                dve.wait_ge(s_pn, i + 1)
                ch.link(dve.tensor_reduce(row_max[0:TN, :], p_n[0:TN, :], AX.X, ALU.max, apply_absolute_value=True))
                ch.link(dve.tensor_scalar(row_max[0:TN, :], row_max[0:TN, :], 2.0 ** -100, None, ALU.max))
                ch.link(dve.tensor_scalar(row_pow[0:TN, :], row_max[0:TN, :].bitcast(I32), 0x7F800000, None, ALU.bitwise_and))
                ch.link(dve.tensor_scalar(row_inv_i[0:TN, :], row_pow[0:TN, :], -1.0, float(254 << 23), ALU.mult, ALU.add))
                dve.tensor_scalar(row_inv[0:TN, :], row_inv_i[0:TN, :].bitcast(F32), 4096.0, None, ALU.mult).then_inc(s_inv, 1)
                dve.wait_ge(s_row_free, i)
                dve.tensor_scalar(row[0:TN, SC:SC + 2].bitcast(F32), row_pow[0:TN, :].bitcast(F32), 1.0 / 4096.0, None, ALU.mult)
                dve.tensor_scalar(row[0:TN, ISC:ISC + 2].bitcast(BF16), row_inv_i[0:TN, 0:1].bitcast(F32).broadcast_to([TN, 2]), 4096.0, None, ALU.mult)
                dve.wait_ge(s_hi, i)
                dve.scalar_tensor_tensor(out=row[0:TN, LO:LO + D], in0=p_n[0:TN, :], scalar=row_inv[0:TN, 0:1],
                                         in1=row[0:TN, HI:HI + D], op0=ALU.mult, op1=ALU.subtract).then_inc(s_row, 1)
                dve.wait_ge(s_row, i)
                dve.sem_inc(s_pn_free, 1)
                dve.wait_ge(s_ps, i + 1)
                dve.tensor_tensor(tile_of(state, t), p_s[0:TN, :], bias[0:TN, l, :], ALU.add).then_inc(s_ps_free, 1)
                assert ch.k == NODE_STEPS

            NODE_STEPS = 4
            dve.wait_ge(s_const, ALL_CONSTS)
            with dve.Fori(0, TILES) as t:
                node(t + 1, 0, t)

            def add_round(r, width):
                dve.wait_ge(s_used, r * SLOTS + 2 * SLOTS)
                dve.tensor_tensor(acc[0:TN, 0:width], acc[0:TN, 0:width], p_acc[0:TN, 0:width], ALU.add).then_inc(s_acc_free, 1)
                dve.wait_ge(s_acc_free, r + 1)

            def relative(t, r, nodes, loaded, before):
                dve.wait_ge(*loaded)
                dve.wait_ge(*before)
                dve.tensor_scalar(rel[:, :], nodes, tile_lo[:, bass.ds(t, 1)], None, ALU.subtract).then_inc(s_dst_free, 1)
                dve.wait_ge(s_dst_free, r + 1)

            def aggregate(ps, t, base, ch):
                ch.link(dve.memset(acc[0:TN, :], 0.0))
                if ps == 0:
                    ch.link(dve.memset(deg[0:TN, :], 0.0))
                q0, q1 = rounds_of(dve, t)
                with dve.Fori(q0, q1) as q:
                    r = q + base
                    relative(t, r, win_dst[:, :], (s_dstw, r * 16), (s_hot, r * SLOTS))
                    for j in range(SLOTS):
                        dve.wait_ge(s_g[j], r * 16)
                        dve.tensor_scalar(hot[:, j, :], node_iota[:, :], rel[:, j:j + 1], slots[:, j, SC:SC + 2].bitcast(F32),
                                          ALU.is_equal, ALU.mult).then_inc(s_hot, 1)
                    add_round(r, D)
                    if ps == 0:
                        dve.tensor_tensor(deg[0:TN, :], deg[0:TN, :], p_deg[0:TN, 0:1], ALU.add).then_inc(s_deg, 1)
                        dve.wait_ge(s_deg, r)
                if ps == 0:
                    ch.link(dve.tensor_scalar(deg[0:TN, :], deg[0:TN, :], 1.0, None, ALU.max))
                    ch.link(dve.reciprocal(inv_deg[0:TN, bass.ds(t, 1)], deg[0:TN, :]))

            def mean_plus_state(t):
                return dve.scalar_tensor_tensor(out=y[0:TN, :], in0=acc[0:TN, :], scalar=inv_deg[0:TN, bass.ds(t, 1)],
                                                in1=tile_of(state, t), op0=ALU.mult, op1=ALU.add)

            STEPS = [4, 1, 5, 4]
            done = [sum(STEPS[:k]) * TILES for k in range(PASSES)]

            def layer_tile(ps, t, base):
                ch = Chain(dve, s_td, t * STEPS[ps] + done[ps])
                aggregate(ps, t, base, ch)
                dve.wait_ge(s_y_free, t + (ps + 1) * TILES + 1)
                mean_plus_state(t).then_inc(s_y, 1)
                dve.wait_ge(s_y, t + ps * TILES + 1)
                assert ch.k == STEPS[ps]

            for ps in range(LAYERS - 1):
                base = rounds_before(dve, ps)
                layer_tile(ps, 0, base)
                with dve.Fori(1, TILES) as t:
                    layer_tile(ps, t, base)
                    node(t + (ps + 1) * TILES, ps + 1, t - 1)
                node((ps + 2) * TILES, ps + 1, TILES - 1)

            def norm(ch, k):
                dve.bn_stats(stats[0:TN, :], y[0:TN, :]).then_inc(s_bn, 1)
                wait_alone(dve, s_bn, k)
                ch.link(dve.bn_aggr(mv[0:TN, :], stats[0:TN, :]))
                dve.tensor_scalar(mv[0:TN, 1:2], mv[0:TN, 1:2], EPS, None, ALU.add).then_inc(s_var, 1)
                dve.wait_ge(s_std, k)
                ch.link(dve.reciprocal(rstd[0:TN, :], std[0:TN, :]))
                return dve.tensor_scalar(h_row[0:TN, :], y[0:TN, :], mv[0:TN, 0:1], rstd[0:TN, 0:1], ALU.subtract, ALU.mult)

            def first_norm_tile(t, base):
                ps = LAYERS - 1
                ch = Chain(dve, s_td, t * STEPS[ps] + done[ps])
                aggregate(ps, t, base, ch)
                ch.link(mean_plus_state(t))
                dve.wait_ge(s_xt, t * 16 + 16 * TILES + 16)
                ch.link(dve.tensor_tensor(y[0:TN, :], y[0:TN, :], xt[0:TN, :], ALU.add))
                dve.sem_inc(s_xt_free, 1)
                dve.wait_ge(s_tp, t + LAYERS * TILES + 1)
                dve.wait_ge(s_keep, t + 1)
                norm(ch, t + 1).then_inc(s_h, 1)
                dve.wait_ge(s_h, t + LAYERS * TILES + 1)
                assert ch.k == STEPS[ps]

            base = rounds_before(dve, LAYERS - 1)
            dve.wait_ge(s_y_free, LAYERS * TILES + 1)
            with dve.Fori(0, TILES) as t:
                first_norm_tile(t, base)

            mch = Chain(dve, s_set_d, ch.k)
            flat = b2_row[:, :, :].rearrange("k a b -> k (a b)")
            part = [b2_part[:, k, :] for k in range(3)]
            for k in range(3):
                mch.link(dve.tensor_copy(part[k], flat))
                if k < 2:
                    mch.link(dve.tensor_tensor(flat, flat, part[k], ALU.subtract))
            parts = b2_parts[:, :, :].rearrange("k a b -> k (a b)")
            mch.link(dve.tensor_scalar(parts, part[0], ident[0:3, 0:1], None, ALU.mult))
            for k in range(1, 3):
                mch.link(dve.scalar_tensor_tensor(out=parts, in0=part[k], scalar=ident[0:3, k:k + 1], in1=parts, op0=ALU.mult, op1=ALU.add))
            mch.link(dve.memset(ones3[:, :], 1.0))

            def hidden(q):
                dve.wait_ge(s_mact, q * 6 + 6)
                dve.wait_ge(s_w, q * NG)
                rows = F * REST
                last = dve.scalar_tensor_tensor(out=filt_h[:, 0:FULL, :], in0=m_exp[:, 0:FULL, :], scalar=-LOG2,
                                                in1=m_relu[:, 0:FULL, :], op0=ALU.add, op1=ALU.add)
                if rows:
                    last = dve.scalar_tensor_tensor(out=filt_h[0:rows, FULL, :], in0=m_exp[0:rows, FULL, :], scalar=-LOG2,
                                                    in1=m_relu[0:rows, FULL, :], op0=ALU.add, op1=ALU.add)
                last.then_inc(s_mh, 1)

            def group(q, r, g):
                j0, n = GROUPS[g]
                dve.wait_ge(s_used, r * SLOTS + j0 + n)
                dve.tensor_tensor(hot32[:, j0:j0 + n, :], node_iota32[:, :].unsqueeze(1).broadcast_to([P, n, TN]),
                                  rel[:, j0:j0 + n].unsqueeze(2).broadcast_to([P, n, TN]), ALU.is_equal)
                dve.wait_ge(s_w, q * NG + g + 1)
                for j in range(n):
                    dve.wait_ge(s_g[j0 + j], r * 16)
                dve.wait_ge(s_av2, q * NG + max(g - 1, 0))
                w = p_w[g % 2][:, 0:n * G].rearrange("p (j k f) -> p j k f", j=n, k=4)
                rows = msg_slots[:, j0:j0 + n, :]
                s = rows[:, :, 0:F]
                v = rows[:, :, F:G].rearrange("p j (c f) -> p j c f", c=C3)
                angle = y_cut[:, j0:j0 + n, 1:YD].unsqueeze(3).broadcast_to([P, n, C3, F])
                dve.tensor_tensor(av[:, g % 2, 0:n, 0:F], s, w[:, :, 0, :], ALU.mult)
                dve.tensor_tensor(av[:, g % 2, 0:n, F:G].rearrange("p j (c f) -> p j c f", c=C3), v,
                                  w[:, :, 3, :].unsqueeze(2).broadcast_to([P, n, C3, F]), ALU.mult).then_inc(s_av, 1)
                dve.tensor_tensor(vy[:, 0:n, :, :], v, angle, ALU.mult).then_inc(s_gd, 1)
                dve.wait_ge(s_m, q * NG + g)
                dve.tensor_tensor(ab[:, 0:n, :], s, w[:, :, 2, :], ALU.mult).then_inc(s_gd, 1)
                dve.wait_ge(s_gd, q * (3 * NG) + 3 * g + 1)
                dve.tensor_reduce(vys[:, 0:n, :], vy[:, 0:n, :, :].rearrange("p j c f -> p j f c"), AX.X, ALU.add).then_inc(s_gd, 1)
                dve.wait_ge(s_gd, q * (3 * NG) + 3 * g + 3)
                msg_free(dve, r, g)
                dve.scalar_tensor_tensor(out=msg[:, g % 2, 0:n, G:G + F], in0=vys[:, 0:n, :], scalar=IS3, in1=w[:, :, 1, :],
                                         op0=ALU.mult, op1=ALU.mult).then_inc(s_w_free, 1)
                dve.tensor_tensor(msg[:, g % 2, 0:n, G + F:2 * G].rearrange("p j (c f) -> p j c f", c=C3),
                                  ab[:, 0:n, :].unsqueeze(2).broadcast_to([P, n, C3, F]), angle, ALU.mult).then_inc(s_m, 1)

            def messages(t, base, ch):
                ch.link(dve.memset(acc[0:TN, :], 0.0))
                q0, q1 = rounds_of(dve, t, meta_m)
                with dve.Fori(q0, q1) as q:
                    r = q + base
                    relative(t, r, win_p[:, :, PAY_SRC].bitcast(I32), (s_src, r * 16), (s_m, q * NG))
                    dve.wait_ge(s_av2, q * NG)
                    dve.tensor_tensor(y_cut[:, :, :], win_p[:, :, PAY_Y:PAY_Y + YD],
                                      win_p[:, :, PAY_C:PAY_C + 1].broadcast_to([P, SLOTS, YD]), ALU.mult).then_inc(s_yw_free, 1)
                    dve.wait_ge(s_yw_free, q + 1)
                    for g in range(NG):
                        group(q, r, g)
                    hidden(q + 1)
                    add_round(r, 2 * G)
                dve.wait_ge(s_ptp, t + 1)
                dve.tensor_copy(pairs[0:TN, :, :].rearrange("p k (h f) -> p k h f", h=2),
                                acc[0:TN, 0:2 * G].rearrange("p (h k f) -> p k h f", h=2, k=4)).then_inc(s_pairs, 1)
                dve.wait_ge(s_pairs, t + 1)

            def output(t, ch):
                dve.wait_ge(s_oact, t * 3 + 3)
                dve.wait_ge(s_o2, t + 1)
                dve.scalar_tensor_tensor(out=o1[:, 0, :], in0=o_exp[:, :], scalar=-LOG2, in1=o_relu[:, :],
                                         op0=ALU.add, op1=ALU.add).then_inc(s_o1s, 1)
                dve.wait_ge(s_o2, t + 2)
                rows = tile_of(state, t)
                dve.scalar_tensor_tensor(out=y[0:TN, 0:B], in0=p_o2[0:TN, 0:B], scalar=RS_B, in1=rows[:, 0:B],
                                         op0=ALU.mult, op1=ALU.add)
                ch.link(dve.scalar_tensor_tensor(out=y[0:TN, B:D].rearrange("p (d c) -> p c d", c=C3),
                                                 in0=p_o2[0:TN, B:D].rearrange("p (c d) -> p c d", c=C3), scalar=RS_B,
                                                 in1=rows[:, B:D].rearrange("p (d c) -> p c d", c=C3), op0=ALU.mult, op1=ALU.add))
                dve.sem_inc(s_o2_free, 1)
                dve.wait_ge(s_outrow_free, t + 1)
                norm(ch, t + TILES + 1).then_inc(s_out, 1)
                dve.wait_ge(s_out, t + 1)

            ps = LAYERS
            base = rounds_before(dve, ps)
            dve.wait_ge(s_tp, (LAYERS + 1) * TILES + 1)
            dve.wait_ge(s_keep, TILES + 1)
            hidden(1)
            messages(0, base, Chain(dve, s_td, done[ps]))
            with dve.Fori(1, TILES) as t:
                ch = Chain(dve, s_td, t * STEPS[ps] + (done[ps] + 1 - STEPS[ps]))
                messages(t, base, ch)
                output(t - 1, ch)
                assert ch.k == STEPS[ps]
            output(TILES - 1, Chain(dve, s_td, done[ps] + 1 + STEPS[ps] * (TILES - 1)))



def kernel(x, src, dst, edge_attr_20, edge_attr_4, edge_weight, L0_gnn_Ws_self, L0_gnn_Ws_neigh, L0_gnn_bs,
           L1_gnn_w_in2f_s, L1_gnn_w_in2f_v, L1_gnn_W1, L1_gnn_b1, L1_gnn_W2, L1_gnn_b2,
           L1_gnn_w_f2o1_s, L1_gnn_w_f2o1_v, L1_gnn_w_f2o2_s, L1_gnn_w_f2o2_v):
    import numpy as np
    import concourse.bacc as bacc
    from concourse.bass_utils import run_bass_kernel_spmd

    def arr(a):
        return np.asarray(a)

    def padded(a, fill):
        a = arr(a)
        return np.concatenate([a, np.full((WIN,) + a.shape[1:], fill, a.dtype)])

    w2 = arr(L1_gnn_W2).reshape(F, F, 6)[:, :, 0:4].transpose(0, 2, 1).reshape(F, 4 * F)
    b2 = arr(L1_gnn_b2).reshape(F, 6)[:, 0:4].T.reshape(4 * F)
    wv = arr(L1_gnn_w_f2o1_v)
    pay = np.zeros((E + WIN, PAY), np.float32)
    pay[0:E, 0:PAY_Y] = arr(edge_attr_20)
    pay[0:E, PAY_Y:PAY_C] = arr(edge_attr_4)
    pay[0:E, PAY_C] = arr(edge_weight)
    pay.view(np.int32)[:, PAY_SRC] = padded(src, N)
    pay.view(np.int32)[:, PAY_DST] = padded(dst, 0)
    arrays = {
        "x": arr(x), "src": padded(src, 0), "dst": padded(dst, N),
        "src_n": padded(src, N)[0:P * CH], "pay": pay,
        "ws": arr(L0_gnn_Ws_self), "wn": arr(L0_gnn_Ws_neigh), "bs": arr(L0_gnn_bs),
        "w_in": np.stack([arr(L1_gnn_w_in2f_s), arr(L1_gnn_w_in2f_v)]),
        "w1": arr(L1_gnn_W1), "b1": arr(L1_gnn_b1), "w2": w2, "b2": b2,
        "wf1": np.stack([arr(L1_gnn_w_f2o1_s), np.concatenate([wv[F:], wv[:F]])]),
        "wf2": np.stack([arr(L1_gnn_w_f2o2_s), arr(L1_gnn_w_f2o2_v)]),
    }
    arrays = {k: np.ascontiguousarray(a) for k, a in arrays.items()}
    nc = bacc.Bacc("TRN2", target_bir_lowering=False, num_devices=1)
    aps = {k: nc.dram_tensor(k, a.shape, mybir.dt.from_np(a.dtype), kind="ExternalInput").ap() for k, a in arrays.items()}
    out = nc.dram_tensor("out", (N, D), F32, kind="ExternalOutput").ap()
    gnn_kernel(nc, out=out, **aps)
    r = run_bass_kernel_spmd(nc, [arrays], core_ids=[0])
    return r.results[0]["out"]
```

```python
from functools import partial

import concourse.bass as bass
from concourse import mybir

F32 = mybir.dt.float32
F16 = mybir.dt.float16
BF16 = mybir.dt.bfloat16
I32 = mybir.dt.int32
ALU = mybir.AluOpType
ACT = mybir.ActivationFunctionType
AX = mybir.AxisListType

P = 128
N, E, D = 3125, 53125, 512
TILES = 25
TN = N // TILES
SLOTS = -(-E // (TILES * P)) + 1
WIN = P * SLOTS
LAYERS = 3
PASSES = LAYERS + 1
EP = 125
EC = E // EP
BLK = 5
NB = EC // BLK
MAXR = -(-E // WIN)
ROUND_MAX = PASSES * TILES * MAXR + 2
BIG = float(1 << 20)
KC = D // P
B, F, R, YD, C3 = 128, 32, 20, 4, 3
PAY_Y, PAY_C, PAY_SRC, PAY_DST, PAY = R, R + YD, R + YD + 1, R + YD + 2, R + YD + 4
CH = -(-E // P)
BINS = TILES + 1
PIECE = 16
PIECES = CH // PIECE
CB = -(-CH // P)
G = 4 * F
HI, LO, SC, ISC, ROW = 0, D, 2 * D, 2 * D + 2, 2 * D + 4
LOG2 = 0.6931471805599453
EPS = 1e-5
HALF = SLOTS // 2
TD0 = 4


class Chain:

    def __init__(self, engine, sem, base=0):
        self.engine, self.sem, self.base, self.k = engine, sem, base, 0

    def link(self, ins):
        self.k += 1
        ins.then_inc(self.sem, 1)
        self.engine.wait_ge(self.sem, self.base + self.k)


def gnn_kernel(nc, x, src, dst, src_n, pay, ws, wn, bs, w_in, w1, b1, w2, b2, wf1, wf2, out):
    def sb(name, shape, dt=F32):
        return nc.alloc_sbuf_tensor(name, shape, dt)

    def pb(name, shape, dt=F32):
        return nc.alloc_psum_tensor(name, shape, dt)

    def sem(name):
        return nc.alloc_semaphore(name)

    tables = [nc.dram_tensor(f"table{i}", [N, ROW], F16).ap() for i in range(LAYERS)]
    msg_table = nc.dram_tensor("msg_table", [N, G], F32).ap()
    chunk_base = nc.dram_tensor("chunk_base", [CB * P, BINS], F32).ap()
    by_src = nc.dram_tensor("by_src", [P * CH + WIN, PAY], F32).ap()

    ident = sb("ident", [P, P])
    iota_i = sb("iota_i", [P, 640], I32)
    node_iota = sb("node_iota", [P, TN], BF16)
    node_iota32 = sb("node_iota32", [P, TN])
    tile_lo = sb("tile_lo", [P, BINS + 1])
    bias = sb("bias", [P, LAYERS, D])
    weights = sb("weights", [P, 2 * LAYERS, KC, D])
    state = sb("state", [P, TILES, D])
    inv_deg = sb("inv_deg", [P, TILES])
    meta = sb("meta", [1, TILES + 1, 4], I32)
    slots = sb("slots", [P, SLOTS, ROW], F16)
    msg_slots = slots[:, :, 0:2 * G].bitcast(F32)
    win_src = sb("win_src", [P, SLOTS], I32)
    win_dst = sb("win_dst", [P, SLOTS], I32)
    gather_idx = sb("gather_idx", [P, SLOTS], I32)
    rel = sb("rel", [P, SLOTS])
    hot = sb("hot", [P, SLOTS, TN], BF16)
    acc = sb("acc", [P, D])
    deg = sb("deg", [P, 1])
    y = sb("y", [P, D])
    h_row = sb("h_row", [P, D])
    h_t = sb("h_t", [P, KC, TN])
    row = sb("row", [P, ROW], F16)
    row_max = sb("row_max", [P, 1])
    row_pow = sb("row_pow", [P, 1], I32)
    row_inv_i = sb("row_inv_i", [P, 1], I32)
    row_inv = sb("row_inv", [P, 1])
    xt = sb("xt", [P, D])
    stats = sb("stats", [P, 6])
    mv = sb("mv", [P, 2])
    rstd = sb("rstd", [P, 1])
    shift = sb("shift", [P, 1])
    msg_row = sb("msg_row", [P, G])
    arena = weights[:, 2:6, :, :].rearrange("p a k n -> p (a k n)")
    taken = [0]

    def reuse(*shape):
        n = 1
        for k in shape:
            n *= k
        part = arena[:, taken[0]:taken[0] + n]
        taken[0] += n
        assert taken[0] <= 4 * KC * D
        names = "abc"[:len(shape)]
        return part.rearrange(f"p ({' '.join(names)}) -> p {' '.join(names)}", **dict(zip(names, shape)))

    hot32 = reuse(SLOTS, TN)
    msg = reuse(2, 4 * 2 * G).rearrange("p h (j k) -> p h j k", j=4)
    m_relu = reuse(5, P)
    m_exp = reuse(5, P)
    filt_h = reuse(5, P)
    win_p = sb("win_p", [P, SLOTS, PAY])
    feat_t = reuse(5, P)
    y_cut = sb("y_cut", [P, SLOTS, YD])
    w_in_sb = sb("w_in_sb", [P, 2, F])
    w1_sb = sb("w1_sb", [4 * PAY, 4 * F])
    b1_sb = sb("b1_sb", [P, 1])
    w2_sb = sb("w2_sb", [P, 4, G])
    b2_row = sb("b2_row", [3, 4, G])
    b2_parts = sb("b2_parts", [3, 4, G], BF16)
    b2_part = sb("b2_part", [3, 3, 4 * G], BF16)
    ones3 = sb("ones3", [3, P], BF16)
    wf1_sb = sb("wf1_sb", [P, 3, B])
    wf2_sb = sb("wf2_sb", [P, 2, B])
    av = sb("av", [P, 2, 4, G])
    ab = sb("ab", [P, 4, F])
    vy = sb("vy", [P, 4, C3, F])
    vys = sb("vys", [P, 4, F])
    pairs = sb("pairs", [P, 4, 2 * F])
    pairs_t = sb("pairs_t", [P, 2, TN])
    o_relu = sb("o_relu", [P, TN])
    o_exp = sb("o_exp", [P, TN])
    o1 = sb("o1", [P, 4, TN])
    src_i = sb("src_i", [P, CH], I32)
    src_f = state[:, 22:23, 0:CH].rearrange("p a c -> p (a c)")
    base_bc = state[:, :, :].rearrange("p a k -> p (a k)")[:, 0:CH * BINS].rearrange("p (c t) -> p c t", t=BINS)
    in_bin = slots[:, :, :].rearrange("p a b -> p (a b)")[:, 0:CH * BINS].bitcast(BF16).rearrange("p (c t) -> p c t", t=BINS)
    GEC = CH // 4
    past = slots[:, :, :].rearrange("p a b -> p (a b)")[:, CH * BINS:CH * BINS + GEC * (BINS + 1)].bitcast(BF16).rearrange("p (c t) -> p c t", t=BINS + 1)
    tri = sb("tri", [P, P], BF16)
    ones = sb("ones", [P, P], BF16)
    tot = sb("tot", [P, CB, BINS], BF16)
    chunk0 = sb("chunk0", [P, CB, BINS])
    totals = sb("totals", [P, BINS])
    scan = sb("scan", [P, 2, BINS])
    start = sb("start", [P, BINS])
    place = sb("place", [P, PIECE, BINS])
    place_f = sb("place_f", [P, CH])
    place_i = sb("place_i", [P, CH], I32)
    scat_idx = sb("scat_idx", [P, 2, PIECE], I32)
    scat_row = sb("scat_row", [P, 2, PIECE, PAY])
    over_m = sb("over_m", [1, TILES, MAXR])
    row_n = sb("row_n", [1, 2, BINS])
    meta_mf = sb("meta_mf", [1, 4, TILES + 1])
    meta_m = sb("meta_m", [1, TILES + 1, 4], I32)
    dst_i = sb("dst_i", [EP, EC], I32)
    dst_f = av[0:EP, :, :, :].rearrange("p a b c -> p (a b c)")[:, 0:EC]
    bmin = sb("bmin", [P, NB])
    bmax = sb("bmax", [P, NB])
    bpos = sb("bpos", [P, NB])
    in_a = slots[0:EP, 0:9, :].rearrange("p a b -> p (a b)")[:, 0:2 * TILES * NB].bitcast(F32).rearrange("p (t b) -> p t b", t=TILES)
    in_b = slots[0:EP, 9:18, :].rearrange("p a b -> p (a b)")[:, 0:2 * TILES * NB].bitcast(F32).rearrange("p (t b) -> p t b", t=TILES)
    ends = sb("ends", [P, 2, TILES])
    ends_t = sb("ends_t", [TILES, 2])
    edge0 = sb("edge0", [TILES, 1])
    edge1 = sb("edge1", [TILES, 1])
    length = sb("length", [TILES, 1])
    steps = sb("steps", [TILES, MAXR])
    over = sb("over", [TILES, MAXR])
    rounds = sb("rounds", [TILES, 1])
    rounds1 = sb("rounds1", [TILES, 1])
    before = sb("before", [TILES, TILES + 1])
    meta_f = sb("meta_f", [1, 4, TILES + 1])

    banks = [pb(f"bank{i}", [P, D]) for i in range(8)]
    p_acc, p_t, p_n, p_s, p_deg = banks[0], banks[1], banks[2], banks[3], banks[4]
    p_mlp_a, p_mlp_b, p_o1, p_o2 = banks[2], banks[3], banks[4], banks[7]
    p_w = [banks[5], banks[6]]
    p_cnt, p_pre, p_rank = banks[5], banks[6], [banks[4], banks[7]]

    s_const = sem("consts_loaded")
    s_iota = sem("iota_made")
    s_dst = sem("dst_loaded")
    s_w0 = sem("first_weights_loaded")
    s_ends = sem("ranges_ready")
    s_meta = sem("meta_ready")
    s_set_d = sem("setup_dve")
    s_set_p = sem("setup_pe")
    s_xt = sem("x_loaded")
    s_xt_free = sem("x_used")
    s_src = sem("win_src_loaded")
    s_dstw = sem("win_dst_loaded")
    s_src_free = sem("win_src_used")
    s_dst_free = sem("win_dst_used")
    s_fw_free = sem("features_used")
    s_yw_free = sem("angles_used")
    s_ftp = sem("features_transposed")
    s_ft = sem("feat_t_ready")
    s_srcn = sem("src_loaded")
    s_bin = sem("bins_ready")
    s_cnt = sem("counted")
    s_tot = sem("tot_ready")
    s_pre = sem("counts_summed")
    s_c0 = sem("chunk0_ready")
    s_c0s = sem("chunk0_stored")
    s_bc = sem("base_loaded")
    s_bc_rest = sem("base_rest_loaded")
    s_tail = sem("tail_stored")
    s_rank = sem("ranked")
    s_rank_free = sem("rank_used")
    s_rank_d = sem("place_dve")
    s_place = sem("places_ready")
    s_pay = [sem("rows_loaded0"), sem("rows_loaded1")]
    s_scat = [sem("scattered0"), sem("scattered1")]
    s_sidx = sem("scat_idx_copied")
    s_idx = sem("idx_copied")
    s_g = [sem(f"gathered{j}") for j in range(SLOTS)]
    s_used = sem("slot_used")
    s_hot = sem("hot_ready")
    s_acc_free = sem("p_acc_free")
    s_y = sem("y_ready")
    s_y_free = sem("y_free")
    s_h = sem("h_ready")
    s_tp = sem("transposed")
    s_ht = sem("h_t_ready")
    s_pn = sem("pn_ready")
    s_ps = sem("ps_ready")
    s_pn_free = sem("pn_free")
    s_ps_free = sem("ps_free")
    s_inv = sem("row_scale_ready")
    s_hi = sem("row_hi_ready")
    s_row = sem("row_ready")
    s_stored = sem("row_stored")
    s_row_free = sem("row_free")
    s_deg = sem("degree_added")
    s_nd = sem("node_dve")
    s_td = sem("tile_dve")
    s_bn = sem("stats_ready")
    s_rstd = sem("rstd_ready")
    s_mv = sem("moments_ready")
    s_var = sem("var_ready")
    s_keep = sem("state_kept")
    s_mrow = sem("msg_row_ready")
    s_mstored = sem("msg_row_stored")
    s_mrow_free = sem("msg_row_free")
    s_gd = sem("group_dve")
    s_mlp = sem("mlp1_ready")
    s_mact = sem("mlp_act")
    s_mh = sem("filter_h_ready")
    s_w = sem("filters_ready")
    s_w_free = sem("filters_used")
    s_av = sem("av_ready")
    s_av2 = sem("av_scaled")
    s_ha = sem("hot_distances")
    s_h32 = sem("hot32_ready")
    s_m = sem("msg_ready")
    s_pairs = sem("pairs_ready")
    s_ptp = sem("pairs_transposed")
    s_pt = sem("pairs_t_ready")
    s_o1 = sem("o1_product")
    s_oact = sem("o_act")
    s_o1v = sem("o1_vectors_ready")
    s_o1s = sem("o1_scalars_ready")
    s_o2 = sem("o2_product")
    s_o2_free = sem("o2_used")
    s_out = sem("out_ready")
    s_outs = sem("out_stored")
    s_outrow_free = sem("out_row_free")


    GROUPS = [(j, min(4, SLOTS - j)) for j in range(0, SLOTS, 4)]
    NG = len(GROUPS)
    ACT_HOTS = (0,)
    NH = len(ACT_HOTS)
    FULL = SLOTS // 4
    REST = SLOTS - 4 * FULL
    RS_B = 1.0 / float(B) ** 0.5
    RS_M = 1.0 / float(2 * F) ** 0.5
    IS3 = 1.0 / 3.0 ** 0.5

    def tile_of(buf, t, rows=TN):
        return buf[0:rows, bass.ds(t, 1), :].rearrange("p a k -> p (a k)")

    def entry(eng, k, c, lo, hi, table=meta):
        return eng.value_load(table[0:1, bass.ds(k, 1), c:c + 1].rearrange("p a k -> p (a k)"), min_val=lo, max_val=hi)

    def rounds_before(eng, ps):
        if ps == 0:
            return 0
        return entry(eng, TILES, 0, 1, TILES * MAXR) * ps

    def rounds_of(eng, t, table=meta):
        return entry(eng, t, 0, 1, TILES * MAXR, table), entry(eng, t, 1, 2, TILES * MAXR + 1, table)

    def walk_rounds(eng, t, base, table, a_round, *steps):
        q0, q1 = rounds_of(eng, t, table)
        a_round(q0, q0 + base, True, *steps)
        with eng.If(q0 + 1 < q1):
            with eng.Fori(q0 + 1, q1) as q:
                a_round(q, q + base, False)

    def wait_alone(eng, sem, value):
        value = eng.to_reg(value)
        eng.wait_ge(s_iota, 11)
        eng.wait_ge(sem, value)

    def msg_free(eng, r, g):
        eng.wait_ge(s_used, r * SLOTS + SLOTS + (sum(GROUPS[g - 2]) if g >= 2 else 0))

    consts = []
    blocks = []
    for l in range(LAYERS):
        consts.append((bias[:, l, :], bass.AP(bs.tensor, l * D, [[0, P], [1, D]])))
        if l:
            consts.append((weights[:, 2 * l, :, :], wn[l, :, :].rearrange("(k p) n -> p k n", p=P)))
            consts.append((weights[:, 2 * l + 1, :, :], ws[l, :, :].rearrange("(k p) n -> p k n", p=P)))
    consts.append((w_in_sb[:, :, :], w_in.rearrange("a b f -> b a f")))
    for j in range(4):
        consts.append((b1_sb[F * j:F * j + F, :], b1.rearrange("(f a) -> f a", a=1)))
        blocks.append((w2_sb[F * j:F * j + F, j, :], w2))
        blocks.append((w1_sb[PAY * j:PAY * j + R, F * j:F * j + F], w1))
        consts.append((b2_row[:, j, :], bass.AP(b2.tensor, 0, [[0, 3], [1, G]])))
    for k in range(3):
        h = 2 * F * (k % 2)
        blocks.append((wf1_sb[h:h + 2 * F, k, :], wf1[min(k, 1), :, :]))
    consts.append((wf2_sb[:, :, :], wf2.rearrange("a b d -> b a d")))
    ALL_CONSTS = 16 * (len(consts) + len(blocks))

    with nc.Block() as block:

        @block.sync
        def _(sp):
            sp.sem_inc(s_row_free, 1)
            sp.sem_inc(s_mrow_free, 1)
            sp.sem_inc(s_outrow_free, 1)
            sp.dma_start(dst_i[:, :], dst[0:E].rearrange("(p c) -> p c", p=EP)).then_inc(s_dst, 16)

            def load_x(t):
                sp.wait_ge(s_y_free, t + 1)
                sp.dma_start(y[0:TN, :], x[bass.ds(t * TN, TN), :]).then_inc(s_xt, 16)

            def store_row(i, ps, t):
                sp.wait_ge(s_row, i)
                sp.dma_start(tables[ps][bass.ds(t * TN, TN), :], row[0:TN, :]).then_inc(s_stored, 16)
                wait_alone(sp, s_stored, i * 16)
                sp.sem_inc(s_row_free, 1)

            sp.dma_start(src_i[:, :], src_n.rearrange("(p c) -> p c", p=P)).then_inc(s_srcn, 16)
            sp.dma_start(by_src[P * CH:P * CH + WIN, :], pay[E:E + WIN, :]).then_inc(s_tail, 16)
            load_x(0)
            sp.dma_start(weights[:, 0, :, :], wn[0, :, :].rearrange("(k p) n -> p k n", p=P)).then_inc(s_w0, 16)
            sp.dma_start(weights[:, 1, :, :], ws[0, :, :].rearrange("(k p) n -> p k n", p=P)).then_inc(s_w0, 16)
            for to, of in consts:
                sp.dma_start(to, of).then_inc(s_const, 16)
            sp.wait_ge(s_iota, 10)
            for to, of in blocks:
                sp.dma_start(to, of).then_inc(s_const, 16)
            sp.wait_ge(s_c0, 1)
            sp.dma_start(chunk_base.rearrange("(b p) t -> p b t", p=P), chunk0[:, :, :]).then_inc(s_c0s, 16)
            sp.wait_ge(s_c0s, 16)
            cut = 2 * PIECE
            for c0, c1, loaded in ((0, cut, s_bc), (cut, CH, s_bc_rest)):
                sp.dma_start(base_bc[:, c0:c1, :].rearrange("p c t -> p (c t)"),
                             bass.AP(chunk_base.tensor, c0 * BINS, [[0, P], [1, (c1 - c0) * BINS]])).then_inc(loaded, 16)
            with sp.Fori(0, TILES - 1) as t:
                load_x(t + 1)
                store_row(t + 1, 0, t)
            store_row(TILES, 0, TILES - 1)

            sp.wait_ge(s_meta, 1)

            def load_windows(ps, t, base, between=None):
                table = meta_m if ps == LAYERS else meta
                q0, _ = rounds_of(sp, t, table)
                e0 = entry(sp, t, 2, 0, E, table)

                def load(q, r, first):
                    e = nc.s_assert_within(e0 + (q - q0) * WIN, 0, E,
                                           skip_runtime_bounds_check_because="a tile's rounds start inside its range of the list")
                    wait_alone(sp, s_src_free, r)
                    if ps < LAYERS:
                        sp.dma_start(win_src[:, :], src[bass.ds(e, WIN)].rearrange("(p j) -> p j", j=SLOTS)).then_inc(s_src, 16)
                    wait_alone(sp, s_dst_free, r)
                    if ps < LAYERS:
                        sp.dma_start(win_dst[:, :], dst[bass.ds(e, WIN)].rearrange("(p j) -> p j", j=SLOTS)).then_inc(s_dstw, 16)
                    else:
                        wait_alone(sp, s_yw_free, q)
                        wait_alone(sp, s_fw_free, q)
                        sp.dma_start(win_p[:, :, :], by_src[bass.ds(e, WIN), :].rearrange("(p j) k -> p j k", j=SLOTS)).then_inc(s_src, 16)
                    if first and between:
                        between()

                walk_rounds(sp, t, base, table, load)

            for ps in range(LAYERS - 1):
                base = rounds_before(sp, ps)
                load_windows(ps, 0, base)
                load_windows(ps, 1, base)
                with sp.Fori(1, TILES - 1) as t:
                    load_windows(ps, t + 1, base, partial(store_row, (ps + 1) * TILES + t, ps + 1, t - 1))
                store_row((ps + 2) * TILES - 1, ps + 1, TILES - 2)
                store_row((ps + 2) * TILES, ps + 1, TILES - 1)

            def load_res(t):
                sp.wait_ge(s_xt_free, t + 1)
                sp.dma_start(xt[0:TN, :], x[bass.ds(t * TN, TN), :]).then_inc(s_xt, 16)

            def store_msg(t):
                sp.wait_ge(s_mrow, t + 1)
                sp.dma_start(msg_table[bass.ds(t * TN, TN), :], msg_row[0:TN, :]).then_inc(s_mstored, 16)
                sp.wait_ge(s_mstored, (t + 1) * 16)
                sp.sem_inc(s_mrow_free, 1)

            base = rounds_before(sp, LAYERS - 1)
            load_windows(LAYERS - 1, 0, base)
            load_res(0)
            load_windows(LAYERS - 1, 1, base)
            with sp.Fori(1, TILES - 1) as t:
                load_windows(LAYERS - 1, t + 1, base, lambda: (load_res(t), store_msg(t - 1)))
            load_res(TILES - 1)
            store_msg(TILES - 2)
            store_msg(TILES - 1)

            def store_out(t):
                sp.wait_ge(s_out, t + 1)
                sp.dma_start(out[bass.ds(t * TN, TN), :], h_row[0:TN, :]).then_inc(s_outs, 16)
                sp.wait_ge(s_outs, (t + 1) * 16)
                sp.sem_inc(s_outrow_free, 1)

            base = rounds_before(sp, LAYERS)
            for half in range(2):
                sp.wait_ge(s_scat[half], 16 * PIECE * PIECES // 2)
            sp.wait_ge(s_tail, 16)
            for t in range(3):
                load_windows(LAYERS, t, base)
            with sp.Fori(2, TILES - 1) as t:
                load_windows(LAYERS, t + 1, base, partial(store_out, t - 2))
            total = entry(sp, TILES, 0, 1, TILES * MAXR, meta_m)
            wait_alone(sp, s_src_free, total + base + 1)
            wait_alone(sp, s_dst_free, total + base + 1)
            wait_alone(sp, s_yw_free, total + 1)
            wait_alone(sp, s_fw_free, total + 1)
            sp.dma_start(win_p[:, :, :], by_src[0:WIN, :].rearrange("(p j) k -> p j k", j=SLOTS)).then_inc(s_src, 16)
            for t in range(TILES - 3, TILES):
                store_out(t)

        @block.gpsimd
        def _(pool):
            pool.sem_inc(s_src_free, 1)
            pool.sem_inc(s_idx, 2)
            pool.iota(iota_i[:, 0:TN], [[1, TN]], base=0, channel_multiplier=0).then_inc(s_iota, 1)
            pool.iota(iota_i[:, 128:128 + BINS + 1], [[TN, BINS + 1]], base=0, channel_multiplier=0).then_inc(s_iota, 1)
            pool.iota(iota_i[:, 160:160 + NB], [[BLK, NB]], base=0, channel_multiplier=EC).then_inc(s_iota, 1)
            pool.iota(iota_i[:, 256:256 + MAXR], [[WIN, MAXR]], base=WIN, channel_multiplier=0).then_inc(s_iota, 1)
            pool.iota(iota_i[:, 300:300 + TILES + 1], [[1, TILES + 1]], base=0, channel_multiplier=-1).then_inc(s_iota, 1)
            pool.memset(ident[:, :], 0.0).then_inc(s_iota, 1)
            pool.wait_ge(s_iota, 6)
            pool.affine_select(out=ident[:, :], in_=ident[:, :], compare_op=ALU.not_equal, fill=1.0,
                               base=0, pattern=[[-1, P]], channel_multiplier=1).then_inc(s_iota, 1)
            pool.memset(w2_sb[:, :, :], 0.0).then_inc(s_iota, 1)
            pool.memset(wf1_sb[:, :, :], 0.0).then_inc(s_iota, 1)
            pool.memset(w1_sb[:, :], 0.0).then_inc(s_iota, 1)
            pool.iota(iota_i[:, 500:500 + P], [[1, P]], base=0, channel_multiplier=-1).then_inc(s_iota, 1)

            pool.wait_ge(s_tail, 16)

            rows = pay[0:P * CH, :].rearrange("(p c) k -> p c k", p=P)

            def load_rows(k, half):
                pool.dma_start(scat_row[:, half, :, :], rows[:, bass.ds(k * PIECE, PIECE), :]).then_inc(s_pay[half], 16)

            def scatter(u, half, last=False):
                k = u * 2 + half
                pool.wait_ge(s_place, k + 1)
                wait_alone(pool, s_pay[half], u * 16 + 16)
                pool.tensor_copy(scat_idx[:, half, :], place_i[:, bass.ds(k * PIECE, PIECE)]).then_inc(s_sidx, 1)
                wait_alone(pool, s_sidx, k + 1)
                for j in range(PIECE):
                    if j == PIECE // 2 and not last:
                        if not isinstance(k, int) or k:
                            wait_alone(pool, s_scat[1 - half], (u + half) * (16 * PIECE))
                        load_rows(k + 1, 1 - half)
                    pool.indirect_dma_start(
                        out=by_src[0:P * CH, :], out_offset=bass.IndirectOffsetOnAxis(ap=scat_idx[:, half, j:j + 1], axis=0),
                        in_=scat_row[:, half, j, :], in_offset=None).then_inc(s_scat[half], 16)

            load_rows(0, 0)
            for half in range(2):
                scatter(0, half)
            with pool.Fori(1, PIECES // 2 - LAYERS) as u:
                for half in range(2):
                    scatter(u, half)

            pool.wait_ge(s_meta, 1)
            for ps in range(PASSES):
                if ps:
                    for half in range(2):
                        scatter(PIECES // 2 - LAYERS - 1 + ps, half, ps == LAYERS and half == 1)
                base = rounds_before(pool, ps)
                if ps < LAYERS:
                    pool.wait_ge(s_stored, 16 * TILES * (ps + 1))
                else:
                    pool.wait_ge(s_mstored, 16 * TILES)
                with pool.Fori(0, TILES) as t:
                    q0, q1 = rounds_of(pool, t, meta_m if ps == LAYERS else meta)
                    with pool.Fori(q0, q1) as q:
                        r = q + base
                        pool.wait_ge(s_src, r * 16)
                        for j in range(SLOTS):
                            if j % HALF == 0:
                                wait_alone(pool, s_used, r * SLOTS + j + HALF)
                                of = win_p[:, j:j + HALF, PAY_DST].bitcast(I32) if ps == LAYERS else win_src[:, j:j + HALF]
                                pool.tensor_copy(gather_idx[:, j:j + HALF], of).then_inc(s_idx, 1)
                                pool.wait_ge(s_idx, r * 2 + 1 + j // HALF)
                                if j:
                                    pool.sem_inc(s_src_free, 1)
                            wait_alone(pool, s_used, r * SLOTS + j + 1)
                            if ps < LAYERS:
                                to, table = slots[:, j, :], tables[ps]
                            else:
                                to, table = slots[:, j, 0:2 * G].bitcast(F32), msg_table
                            pool.indirect_dma_start(
                                out=to, out_offset=None, in_=table[:, :],
                                in_offset=bass.IndirectOffsetOnAxis(ap=gather_idx[:, j:j + 1], axis=0),
                            ).then_inc(s_g[j], 16)

        @block.tensor
        def _(pe):
            pe.sem_inc(s_used, 2 * SLOTS)
            pe.sem_inc(s_fw_free, 1)
            for s in (s_tp, s_pn, s_ps, s_ptp, s_o1, s_o2, s_ftp, s_mlp):
                pe.sem_inc(s, 1)
            pe.sem_inc(s_w, NG)
            pe.wait_ge(s_iota, 7)
            pe.wait_ge(s_bin, 1)
            for b in range(CB):
                n = min(P, CH - b * P)
                for k in range(BINS):
                    last = pe.matmul(p_cnt[0:n, b * BINS + k:b * BINS + k + 1], in_bin[:, b * P:b * P + n, k], ones[:, 0:1], start=True, stop=True)
            last.then_inc(s_cnt, 1)
            pe.wait_ge(s_tot, 1)
            for b in range(CB):
                for a in range(b):
                    pe.matmul(p_pre[:, b * BINS:(b + 1) * BINS], ones[:, :], tot[:, a, :], start=a == 0, stop=False)
                pe.matmul(p_pre[:, b * BINS:(b + 1) * BINS], tri[:, :], tot[:, b, :], start=b == 0, stop=True)
            for a in range(CB):
                last = pe.matmul(p_pre[:, 256:256 + BINS], ones[:, :], tot[:, a, :], start=a == 0, stop=a == CB - 1)
            last.then_inc(s_pre, 1)
            with pe.Fori(0, PIECES // 2) as u:
                for half in range(2):
                    k = u * 2 + half
                    pe.wait_ge(s_rank_free, k + 1)
                    pe.matmul(p_rank[half][:, 0:PIECE * BINS], tri[:, :],
                              in_bin[:, bass.ds(k * PIECE, PIECE), :].rearrange("p c t -> p (c t)"), start=True, stop=True).then_inc(s_rank, 1)
            pe.wait_ge(s_ends, 1)
            for k in range(2):
                last = pe.transpose(p_t[0:TILES, k * P:k * P + EP], ends[0:EP, k, :], ident[0:EP, 0:EP])
            last.then_inc(s_set_p, 1)
            pe.wait_ge(s_ends, 2)
            pe.matmul(p_n[0:1, 0:TILES + 1], rounds[:, :], before[:, :], start=True, stop=True)
            pe.matmul(p_n[0:1, 32:32 + TILES], rounds[:, :], ident[0:TILES, 0:TILES], start=True, stop=True)
            pe.matmul(p_n[0:1, 64:64 + TILES], edge0[:, :], ident[0:TILES, 0:TILES], start=True, stop=True).then_inc(s_set_p, 1)
            pe.wait_ge(s_meta, 1)

            def node(i, l):
                pe.wait_ge(s_h, i)
                pe.wait_ge(s_ht, i)
                for k in range(KC):
                    last = pe.transpose(p_t[:, k * P:k * P + TN], h_row[0:TN, k * P:(k + 1) * P], ident[0:TN, 0:TN])
                last.then_inc(s_tp, 1)
                pe.wait_ge(s_ht, i + 1)
                pe.wait_ge(s_pn_free, i)
                for k in range(KC):
                    last = pe.matmul(p_n[0:TN, :], h_t[:, k, :], weights[:, 2 * l, k, :], start=k == 0, stop=k == KC - 1)
                last.then_inc(s_pn, 1)
                pe.wait_ge(s_ps_free, i)
                for k in range(KC):
                    last = pe.matmul(p_s[0:TN, :], h_t[:, k, :], weights[:, 2 * l + 1, k, :], start=k == 0, stop=k == KC - 1)
                last.then_inc(s_ps, 1)

            def aggregate(ps, t, base, *steps):
                def sums(q, r, first_round, step=None):
                    pe.wait_ge(s_acc_free, r)
                    for j in range(SLOTS):
                        if j == HALF and step:
                            step()
                        pe.wait_ge(s_hot, r * SLOTS + j + 1)
                        first, end = j == 0, j == SLOTS - 1
                        if ps == 0:
                            pe.matmul(p_deg[0:TN, 0:1], hot[:, j, :], slots[:, j, ISC:ISC + 1].bitcast(BF16), start=first, stop=end)
                        pe.matmul(p_acc[0:TN, :], hot[:, j, :], slots[:, j, HI:HI + D], start=first, stop=False)
                        pe.matmul(p_acc[0:TN, :], hot[:, j, :], slots[:, j, LO:LO + D], start=False, stop=end).then_inc(s_used, 1)

                walk_rounds(pe, t, base, meta, sums, *steps)

            pe.wait_ge(s_w0, 32)
            with pe.Fori(0, TILES) as t:
                node(t + 1, 0)
            pe.wait_ge(s_const, ALL_CONSTS)
            for ps in range(LAYERS - 1):
                base = rounds_before(pe, ps)
                aggregate(ps, 0, base)
                with pe.Fori(1, TILES) as t:
                    aggregate(ps, t, base, partial(node, (ps + 1) * TILES + t, ps + 1))
                node((ps + 2) * TILES, ps + 1)

            def msg_node(t):
                i = LAYERS * TILES + t + 1
                pe.wait_ge(s_h, i)
                pe.wait_ge(s_ht, i)
                for k in range(4):
                    cols = h_row[0:TN, 0:B] if k == 0 else h_row[0:TN, B:4 * B].rearrange("p (b c) -> p c b", c=C3)[:, k - 1, :]
                    last = pe.transpose(p_t[:, k * P:k * P + TN], cols, ident[0:TN, 0:TN])
                last.then_inc(s_tp, 1)
                pe.wait_ge(s_ht, i + 1)
                pe.wait_ge(s_pn_free, i)
                for k in range(4):
                    last = pe.matmul(p_n[0:TN, k * F:(k + 1) * F], h_t[:, k, :], w_in_sb[:, min(k, 1), :], start=True, stop=True)
                last.then_inc(s_pn, 1)

            base = rounds_before(pe, LAYERS - 1)
            aggregate(LAYERS - 1, 0, base)
            with pe.Fori(1, TILES) as t:
                aggregate(LAYERS - 1, t, base)
                msg_node(t - 1)
            msg_node(TILES - 1)
            pe.wait_ge(s_pn_free, (LAYERS + 1) * TILES + 1)

            def features(q, r):
                wait_alone(pe, s_src, r * 16)
                wait_alone(pe, s_mact, q * 6)
                for g, (j0, n) in enumerate(GROUPS):
                    o = p_t[0:n * PAY, g * P:(g + 1) * P] if g < FULL else p_mlp_b[0:n * PAY, P:2 * P]
                    last = pe.transpose(o, win_p[:, j0:j0 + n, :].rearrange("p j k -> p (j k)"), ident[:, :])
                last.then_inc(s_ftp, 1)
                pe.wait_ge(s_ftp, q + 1)
                pe.sem_inc(s_fw_free, 1)

            def hidden(q):
                pe.wait_ge(s_ft, q)
                pe.wait_ge(s_mact, q * 6)
                for g, (j0, n) in enumerate(GROUPS):
                    o = p_mlp_a[0:n * F, g * P:(g + 1) * P] if g < FULL else p_mlp_b[0:n * F, 0:P]
                    last = pe.matmul(o, w1_sb[0:n * PAY, 0:n * F], feat_t[0:n * PAY, g, :], start=True, stop=True)
                last.then_inc(s_mlp, 1)

            def filters(q, g):
                j0, n = GROUPS[g]
                pe.wait_ge(s_w_free, q * NG + max(g - 1, 0))
                w = p_w[g % 2]
                pe.matmul(w[:, 0:n * G], ones3[:, :], b2_parts[:, 0:n, :].rearrange("k a b -> k (a b)"),
                          start=True, stop=False)
                pe.matmul(w[:, 0:n * G], filt_h[0:n * F, g, :], w2_sb[0:n * F, 0:n, :].rearrange("k a b -> k (a b)"),
                          start=False, stop=True).then_inc(s_w, 1)

            def output_t(t):
                pe.wait_ge(s_pairs, t + 1)
                pe.wait_ge(s_pt, t + 1)
                for k in range(2):
                    last = pe.transpose(p_t[:, k * P:k * P + TN], pairs[0:TN, 2 * k:2 * k + 2, :].rearrange("p a b -> p (a b)"), ident[0:TN, 0:TN])
                last.then_inc(s_ptp, 1)

            def output_1(t):
                pe.wait_ge(s_pt, t + 2)
                pe.wait_ge(s_o1v, t + 1)
                for k, w in enumerate((0, 1, 2, 1)):
                    last = pe.matmul(p_o1[:, k * P:k * P + TN], wf1_sb[:, w, :], pairs_t[:, k // 2, :], start=True, stop=True)
                last.then_inc(s_o1, 1)

            def output_2(t):
                pe.wait_ge(s_o1v, t + 2)
                pe.wait_ge(s_o1s, t + 2)
                pe.wait_ge(s_o2_free, t + 1)
                for k in range(4):
                    last = pe.matmul(p_o2[0:TN, k * P:(k + 1) * P], o1[:, k, :], wf2_sb[:, min(k, 1), :], start=True, stop=True)
                last.then_inc(s_o2, 1)

            def message_round(q, r, first, t_out=None):
                pe.wait_ge(s_mh, q + 1)
                filters(q, 0)
                pe.wait_ge(s_acc_free, r)
                for g, (j0, n) in enumerate(GROUPS):
                    if g + 1 < NG:
                        filters(q, g + 1)
                    if t_out is not None and g < 2:
                        (output_t, output_1)[g](t_out)
                    if g == 1:
                        features(q + 1, r + 1)
                    if g == 2:
                        hidden(q + 1)
                    pe.wait_ge(s_m, q * NG + g + 1)
                    pe.wait_ge(s_av2, q * NG + g + 1)
                    if g in ACT_HOTS:
                        pe.wait_ge(s_h32, q * NH + ACT_HOTS.index(g) + 1)
                    for j in range(n):
                        pe.matmul(p_acc[0:TN, 0:2 * G], hot32[:, j0 + j, :], msg[:, g % 2, j, :],
                                  start=j0 + j == 0, stop=j0 + j == SLOTS - 1).then_inc(s_used, 1)
                if t_out is not None:
                    output_2(t_out)

            base = rounds_before(pe, LAYERS)
            features(1, base + 1)
            hidden(1)
            walk_rounds(pe, 0, base, meta_m, message_round)
            with pe.Fori(1, TILES) as t:
                walk_rounds(pe, t, base, meta_m, message_round, t - 1)
            for step in (output_t, output_1, output_2):
                step(TILES - 1)

        @block.scalar
        def _(act):
            for s in (s_y_free, s_ht, s_keep, s_pt, s_o1v):
                act.sem_inc(s, 1)
            act.sem_inc(s_mact, 6)
            act.sem_inc(s_av2, NG)
            act.sem_inc(s_h32, NH)
            act.sem_inc(s_ha, NH)

            def transposed(i):
                act.wait_ge(s_tp, i + 1)
                act.wait_ge(s_pn, i)
                act.activation(h_t[:, :, :], p_t[:, :].rearrange("p (k n) -> p k n", k=KC)[:, :, 0:TN], ACT.Copy).then_inc(s_ht, 1)

            def node(i):
                act.wait_ge(s_ps, i)
                transposed(i)
                act.wait_ge(s_inv, i)
                act.wait_ge(s_row_free, i)
                act.activation(row[0:TN, HI:HI + D], p_n[0:TN, :], ACT.Copy, scale=row_inv[0:TN, 0:1]).then_inc(s_hi, 1)

            def rows_in(i, func):
                act.wait_ge(s_tp, i)
                act.activation(h_row[0:TN, :], y[0:TN, :], func).then_inc(s_h, 1)
                act.wait_ge(s_h, i)
                act.sem_inc(s_y_free, 1)

            with act.Fori(0, TILES) as t:
                act.wait_ge(s_xt, t * 16 + 16)
                rows_in(t + 1, ACT.Copy)
                node(t + 1)
            for ps in range(LAYERS - 1):
                i0 = (ps + 1) * TILES
                act.wait_ge(s_y, ps * TILES + 1)
                rows_in(i0 + 1, ACT.Relu)
                with act.Fori(1, TILES) as t:
                    node(t + i0)
                    act.wait_ge(s_y, t + ps * TILES + 1)
                    rows_in(t + i0 + 1, ACT.Relu)
                node(i0 + TILES)
            act.wait_ge(s_ps, LAYERS * TILES + 1)

            act.preload_act_table_set("natural_log_exp_and_others")

            def root(k):
                act.wait_ge(s_var, k)
                act.activation(rstd[0:TN, :], mv[0:TN, 1:2], ACT.Ln).then_inc(s_rstd, 1)
                act.wait_ge(s_rstd, (k - 1) * 2 + 1)
                act.activation(rstd[0:TN, :], rstd[0:TN, :], ACT.Exp, scale=-0.5).then_inc(s_rstd, 1)

            def keep(t):
                act.wait_ge(s_h, t + LAYERS * TILES + 1)
                act.activation(tile_of(state, t), h_row[0:TN, :], ACT.Copy).then_inc(s_keep, 1)

            def msg_node(t):
                i = t + LAYERS * TILES + 1
                transposed(i)
                act.wait_ge(s_pn, i + 1)
                act.wait_ge(s_mrow_free, t + 1)
                act.activation(msg_row[0:TN, :], p_n[0:TN, 0:G], ACT.Copy, scale=RS_B).then_inc(s_mrow, 1)
                act.wait_ge(s_mrow, t + 1)
                act.sem_inc(s_pn_free, 1)

            root(1)
            keep(0)
            with act.Fori(1, TILES) as t:
                msg_node(t - 1)
                root(t + 1)
                keep(t)
            msg_node(TILES - 1)

            def hidden(q):
                act.wait_ge(s_mlp, q + 1)
                act.wait_ge(s_mh, q)
                rows = F * REST
                parts = [(p_mlp_a[:, :], slice(0, P), slice(0, FULL)), (p_mlp_b[0:rows, 0:P], slice(0, rows), slice(FULL, FULL + 1))]
                parts = [(a, b, c) for a, b, c in parts if b.stop]
                for a, b, c in parts:
                    act.activation(m_relu[b, c, :].rearrange("p g e -> p (g e)"), a, ACT.Relu, bias=b1_sb[b, :])
                for a, b, c in parts:
                    act.activation(m_exp[b, c, :].rearrange("p g e -> p (g e)"), a, ACT.Abs, bias=b1_sb[b, :]).then_inc(s_mact, 1)
                act.wait_ge(s_mact, q * 6 + 2)
                for _, b, c in parts:
                    act.activation(m_exp[b, c, :], m_exp[b, c, :], ACT.Exp, scale=-1.0).then_inc(s_mact, 1)
                act.wait_ge(s_mact, q * 6 + 4)
                for _, b, c in parts:
                    act.activation(m_exp[b, c, :], m_exp[b, c, :], ACT.Ln, bias=1.0).then_inc(s_mact, 1)

            def features(q):
                act.wait_ge(s_ftp, q + 1)
                act.wait_ge(s_mlp, q)
                act.activation(feat_t[0:4 * PAY, 0:FULL, :], p_t[0:4 * PAY, 0:FULL * P].rearrange("p (g e) -> p g e", g=FULL), ACT.Copy)
                last = act.activation(feat_t[0:REST * PAY, FULL, :], p_mlp_b[0:REST * PAY, P:2 * P], ACT.Copy)
                last.then_inc(s_ft, 1)

            def distances(q, r, g):
                j0, n = GROUPS[g]
                act.wait_ge(s_dst_free, r + 1)
                act.wait_ge(s_used, r * SLOTS + j0 + n)
                for j in range(j0, j0 + n):
                    last = act.activation(hot32[:, j, :], node_iota32[:, :], ACT.Abs, bias=rel[:, j:j + 1], scale=-1.0)
                last.then_inc(s_ha, 1)

            def one_hots(q, g):
                j0, n = GROUPS[g]
                act.wait_ge(s_ha, q * NH + ACT_HOTS.index(g) + 1)
                act.activation(hot32[:, j0:j0 + n, :], hot32[:, j0:j0 + n, :], ACT.Relu, bias=1.0, scale=-1.0).then_inc(s_h32, 1)

            def scaled(q, r, g):
                j0, n = GROUPS[g]
                act.wait_ge(s_av, q * NG + g + 1)
                msg_free(act, r, g)
                for j in range(n):
                    last = act.activation(msg[:, g % 2, j, 0:G], av[:, g % 2, j, :], ACT.Copy, scale=y_cut[:, j0 + j, 0:1])
                last.then_inc(s_av2, 1)

            def output_t(t):
                act.wait_ge(s_ptp, t + 2)
                act.wait_ge(s_o1, t + 1)
                act.activation(pairs_t[:, :, :], p_t[:, 0:2 * P].rearrange("p (k n) -> p k n", k=2)[:, :, 0:TN], ACT.Copy).then_inc(s_pt, 1)

            def output_1(t):
                act.wait_ge(s_o1, t + 2)
                act.wait_ge(s_o1s, t + 1)
                act.activation(o_relu[:, :], p_o1[:, 0:TN], ACT.Relu, scale=RS_M)
                act.activation(o_exp[:, :], p_o1[:, 0:TN], ACT.Abs, scale=RS_M).then_inc(s_oact, 1)
                act.wait_ge(s_o2, t + 1)
                act.activation(o1[:, 1:4, :], p_o1[:, P:4 * P].rearrange("p (k n) -> p k n", k=3)[:, :, 0:TN], ACT.Copy, scale=RS_M).then_inc(s_o1v, 1)

            def output_exp(t):
                act.wait_ge(s_oact, t * 3 + 1)
                act.activation(o_exp[:, :], o_exp[:, :], ACT.Exp, scale=-1.0).then_inc(s_oact, 1)

            def output_ln(t):
                act.wait_ge(s_oact, t * 3 + 2)
                act.activation(o_exp[:, :], o_exp[:, :], ACT.Ln, bias=1.0).then_inc(s_oact, 1)

            output_steps = (output_t, output_1, output_exp, output_ln)

            def message_round(q, r, first, t_out=None, t_norm=None):
                if 0 in ACT_HOTS:
                    distances(q, r, 0)
                    one_hots(q, 0)
                for g in range(NG):
                    if g == 2:
                        features(q + 1)
                    if g == 4:
                        hidden(q + 1)
                    scaled(q, r, g)
                    if g + 1 in ACT_HOTS:
                        distances(q, r, g + 1)
                        one_hots(q, g + 1)
                    if t_out is not None and g < 4:
                        output_steps[g](t_out)
                    if t_norm is not None and g == 2:
                        root(t_norm + TILES + 1)

            base = rounds_before(act, LAYERS)
            features(1)
            hidden(1)
            walk_rounds(act, 0, base, meta_m, message_round)
            walk_rounds(act, 1, base, meta_m, message_round, 0)
            with act.Fori(2, TILES) as t:
                walk_rounds(act, t, base, meta_m, message_round, t - 1, t - 2)
            root(2 * TILES - 1)
            for step in output_steps:
                step(TILES - 1)
            root(2 * TILES)

        @block.vector
        def _(dve):
            for s in (s_dst_free, s_acc_free, s_pn_free, s_ps_free, s_xt_free, s_yw_free, s_mh, s_o1s, s_o2_free):
                dve.sem_inc(s, 1)
            dve.sem_inc(s_hot, SLOTS)
            dve.sem_inc(s_deg, 1)
            dve.sem_inc(s_td, TD0)
            for s in (s_w_free, s_av, s_m):
                dve.sem_inc(s, NG)
            dve.sem_inc(s_rank_free, 2)
            dve.sem_inc(s_rank_d, 1)
            dve.sem_inc(s_gd, 3 * NG)
            ch = Chain(dve, s_set_d)
            dve.wait_ge(s_iota, 11)
            dve.tensor_copy(node_iota[:, :], iota_i[:, 0:TN])
            dve.tensor_copy(node_iota32[:, :], iota_i[:, 0:TN])
            dve.tensor_copy(tile_lo[:, :], iota_i[:, 128:128 + BINS + 1])
            dve.tensor_scalar(tri[:, :], iota_i[:, 500:500 + P], 0.0, None, ALU.is_gt)
            dve.memset(ones[:, :], 1.0)
            dve.memset(tot[:, :, :], 0.0)
            dve.tensor_copy(bpos[:, :], iota_i[:, 160:160 + NB])
            dve.tensor_copy(steps[:, :], iota_i[0:TILES, 256:256 + MAXR])
            ch.link(dve.tensor_scalar(before[:, :], iota_i[0:TILES, 300:300 + TILES + 1], 0.0, None, ALU.is_gt))
            dve.wait_ge(s_srcn, 16)
            ch.link(dve.tensor_copy(src_f, src_i[:, :]))
            for c in range(0, CH, GEC):
                ch.link(dve.tensor_tensor(past, src_f[:, c:c + GEC].unsqueeze(2).broadcast_to([P, GEC, BINS + 1]),
                                          tile_lo[:, :].unsqueeze(1).broadcast_to([P, GEC, BINS + 1]), ALU.is_ge))
                ch.link(dve.tensor_tensor(in_bin[:, c:c + GEC, :], past[:, :, 0:BINS], past[:, :, 1:BINS + 1], ALU.subtract))
            dve.sem_inc(s_bin, 1)
            dve.wait_ge(s_cnt, 1)
            for b in range(CB):
                n = min(P, CH - b * P)
                last = dve.tensor_copy(tot[0:n, b, :], p_cnt[0:n, b * BINS:(b + 1) * BINS])
            last.then_inc(s_tot, 1)
            dve.wait_ge(s_pre, 1)
            ch.link(dve.tensor_copy(totals[:, :], p_pre[:, 256:256 + BINS]))

            def prefix(bufs, of, n, end):
                ch.link(dve.tensor_copy(bufs[0], of))
                d, k = 1, 0
                while d < n:
                    dve.tensor_copy(bufs[1 - k][:, 0:d], bufs[k][:, 0:d])
                    ch.link(dve.tensor_tensor(bufs[1 - k][:, d:n], bufs[k][:, d:n], bufs[k][:, 0:n - d], ALU.add))
                    d, k = 2 * d, 1 - k
                ch.link(dve.tensor_tensor(end, bufs[k], of, ALU.subtract))

            prefix([scan[:, 0, :], scan[:, 1, :]], totals[:, :], BINS, start[:, :])
            dve.tensor_tensor(chunk0[:, :, :], p_pre[:, 0:CB * BINS].rearrange("p (b t) -> p b t", b=CB),
                              start[:, :].unsqueeze(1).broadcast_to([P, CB, BINS]), ALU.add).then_inc(s_c0, 1)
            ch.link(dve.tensor_tensor(over_m[:, :, :], totals[0:1, 0:TILES].unsqueeze(2).broadcast_to([1, TILES, MAXR]),
                                      steps[0:1, :].unsqueeze(1).broadcast_to([1, TILES, MAXR]), ALU.is_gt))
            ch.link(dve.memset(meta_mf[:, :, :], 0.0))
            ch.link(dve.tensor_reduce(meta_mf[:, 3, 0:TILES], over_m[:, :, :], AX.X, ALU.add))
            ch.link(dve.tensor_scalar(meta_mf[:, 3, 0:TILES], meta_mf[:, 3, 0:TILES], 1.0, None, ALU.add))
            prefix([row_n[:, 0, :], row_n[:, 1, :]], meta_mf[:, 3, :], TILES + 1, meta_mf[:, 0, :])
            ch.link(dve.tensor_copy(meta_m[:, TILES, 0:1], meta_mf[:, 0, TILES:TILES + 1]))
            ch.link(dve.tensor_scalar(meta_mf[:, 0, :], meta_mf[:, 0, :], 1.0, None, ALU.add))
            ch.link(dve.tensor_tensor(meta_mf[:, 1, 0:TILES], meta_mf[:, 0, 0:TILES], meta_mf[:, 3, 0:TILES], ALU.add))
            ch.link(dve.tensor_copy(meta_mf[:, 2, 0:TILES], start[0:1, 0:TILES]))
            ch.link(dve.tensor_copy(meta_m[:, 0:TILES, 0:3], meta_mf[:, 0:3, 0:TILES].rearrange("p a t -> p t a")))

            dve.wait_ge(s_bc, 16)
            def places(k, half):
                part = bass.ds(k * PIECE, PIECE)
                dve.wait_ge(s_rank, k + 1)
                dve.tensor_tensor(place[:, :, :], p_rank[half][:, 0:PIECE * BINS].rearrange("p (c t) -> p c t", t=BINS),
                                  base_bc[:, part, :], ALU.add).then_inc(s_rank_free, 1)
                dve.wait_ge(s_rank_free, k + 3)
                dve.tensor_tensor(place[:, :, :], place[:, :, :], in_bin[:, part, :], ALU.mult).then_inc(s_rank_d, 1)
                dve.wait_ge(s_rank_d, k * 2 + 2)
                dve.tensor_reduce(place_f[:, part], place[:, :, :], AX.X, ALU.add).then_inc(s_rank_d, 1)
                dve.wait_ge(s_rank_d, k * 2 + 3)
                dve.tensor_copy(place_i[:, part], place_f[:, part]).then_inc(s_place, 1)

            for k in range(2):
                places(k, k)
            dve.wait_ge(s_bc_rest, 16)
            with dve.Fori(1, PIECES // 2) as u:
                for half in range(2):
                    places(u * 2 + half, half)
            dve.wait_ge(s_place, PIECES)
            dve.wait_ge(s_dst, 16)
            ch.link(dve.tensor_copy(dst_f, dst_i[:, :]))
            blocks = dst_f.rearrange("p (b e) -> p b e", e=BLK)
            dve.tensor_reduce(bmin[0:EP, :], blocks, AX.X, ALU.min)
            ch.link(dve.tensor_reduce(bmax[0:EP, :], blocks, AX.X, ALU.max))
            lo = tile_lo[0:EP, 0:TILES].unsqueeze(2).broadcast_to([EP, TILES, NB])
            pos = bpos[0:EP, :].unsqueeze(1).broadcast_to([EP, TILES, NB])
            ch.link(dve.tensor_tensor(in_a, bmax[0:EP, :].unsqueeze(1).broadcast_to([EP, TILES, NB]), lo, ALU.is_ge))
            ch.link(dve.tensor_scalar(bmin[0:EP, :], bmin[0:EP, :], float(TN - 1), None, ALU.subtract))
            ch.link(dve.tensor_tensor(in_b, bmin[0:EP, :].unsqueeze(1).broadcast_to([EP, TILES, NB]), lo, ALU.is_le))
            ch.link(dve.tensor_tensor(in_a, in_a, in_b, ALU.mult))
            ch.link(dve.tensor_scalar(in_a, in_a, BIG, None, ALU.mult))
            ch.link(dve.tensor_tensor(in_b, pos, in_a, ALU.subtract))
            dve.tensor_reduce(ends[0:EP, 0, :], in_b, AX.X, ALU.min)
            ch.link(dve.tensor_tensor(in_a, pos, in_a, ALU.add))
            dve.tensor_reduce(ends[0:EP, 1, :], in_a, AX.X, ALU.max).then_inc(s_ends, 1)
            dve.wait_ge(s_set_p, 1)
            dve.tensor_reduce(edge0[:, :], p_t[0:TILES, 0:EP], AX.X, ALU.min)
            ch.link(dve.tensor_reduce(edge1[:, :], p_t[0:TILES, P:P + EP], AX.X, ALU.max))
            ch.link(dve.tensor_scalar(edge0[:, :], edge0[:, :], BIG, float(E), ALU.add, ALU.min))
            ch.link(dve.tensor_scalar(edge1[:, :], edge1[:, :], BIG - BLK, None, ALU.subtract))
            ch.link(dve.tensor_tensor(length[:, :], edge1[:, :], edge0[:, :], ALU.subtract))
            ch.link(dve.tensor_scalar(over[:, :], steps[:, :], length[:, 0:1], None, ALU.is_lt))
            ch.link(dve.tensor_reduce(rounds[:, :], over[:, :], AX.X, ALU.add))
            ch.link(dve.tensor_scalar(rounds[:, :], rounds[:, :], 1.0, None, ALU.add))
            dve.sem_inc(s_ends, 1)
            dve.wait_ge(s_set_p, 2)
            dve.tensor_copy(meta_f[:, 2, 0:TILES], p_n[0:1, 64:64 + TILES])
            dve.tensor_copy(meta_f[:, 3, 0:TILES], p_n[0:1, 32:32 + TILES])
            ch.link(dve.tensor_scalar(meta_f[:, 0, :], p_n[0:1, 0:TILES + 1], 1.0, None, ALU.add))
            ch.link(dve.tensor_tensor(meta_f[:, 1, 0:TILES], meta_f[:, 0, 0:TILES], meta_f[:, 3, 0:TILES], ALU.add))
            ch.link(dve.tensor_copy(meta[:, 0:TILES, 0:3], meta_f[:, 0:3, 0:TILES].rearrange("p a t -> p t a")))
            ch.link(dve.tensor_copy(meta[:, TILES, 0:1], p_n[0:1, TILES:TILES + 1]))
            dve.sem_inc(s_meta, 1)

            def table_rows(i, l, t):
                ch = Chain(dve, s_nd, (i - 1) * NODE_STEPS)
                dve.wait_ge(s_pn, i + 1)
                ch.link(dve.tensor_reduce(row_max[0:TN, :], p_n[0:TN, :], AX.X, ALU.max, apply_absolute_value=True))
                ch.link(dve.tensor_scalar(row_max[0:TN, :], row_max[0:TN, :], 2.0 ** -100, None, ALU.max))
                ch.link(dve.tensor_scalar(row_pow[0:TN, :], row_max[0:TN, :].bitcast(I32), 0x7F800000, None, ALU.bitwise_and))
                ch.link(dve.tensor_scalar(row_inv_i[0:TN, :], row_pow[0:TN, :], -1.0, float(254 << 23), ALU.mult, ALU.add))
                dve.tensor_scalar(row_inv[0:TN, :], row_inv_i[0:TN, :].bitcast(F32), 4096.0, None, ALU.mult).then_inc(s_inv, 1)
                dve.wait_ge(s_row_free, i)
                dve.tensor_scalar(row[0:TN, SC:SC + 2].bitcast(F32), row_pow[0:TN, :].bitcast(F32), 1.0 / 4096.0, None, ALU.mult)
                dve.tensor_scalar(row[0:TN, ISC:ISC + 2].bitcast(BF16), row_inv_i[0:TN, 0:1].bitcast(F32).broadcast_to([TN, 2]), 4096.0, None, ALU.mult)
                dve.wait_ge(s_hi, i)
                dve.scalar_tensor_tensor(out=row[0:TN, LO:LO + D], in0=p_n[0:TN, :], scalar=row_inv[0:TN, 0:1],
                                         in1=row[0:TN, HI:HI + D], op0=ALU.mult, op1=ALU.subtract).then_inc(s_row, 1)
                dve.wait_ge(s_row, i)
                dve.sem_inc(s_pn_free, 1)
                assert ch.k == NODE_STEPS

            def own_part(i, l, t):
                dve.wait_ge(s_ps, i + 1)
                dve.tensor_tensor(tile_of(state, t), p_s[0:TN, :], bias[0:TN, l, :], ALU.add).then_inc(s_ps_free, 1)

            def node(i, l, t):
                table_rows(i, l, t)
                own_part(i, l, t)

            NODE_STEPS = 4
            CLOSE_AT, TABLE_AT, OWN_AT = 3, 13, 15
            dve.wait_ge(s_const, ALL_CONSTS)
            with dve.Fori(0, TILES) as t:
                node(t + 1, 0, t)

            def add_round(following, width):
                dve.wait_ge(s_used, following * SLOTS + SLOTS)
                dve.tensor_tensor(acc[0:TN, 0:width], acc[0:TN, 0:width], p_acc[0:TN, 0:width], ALU.add).then_inc(s_acc_free, 1)
                wait_alone(dve, s_acc_free, following)

            def relative(t, r, nodes, loaded, *before):
                dve.wait_ge(*loaded)
                for sem_and_value in before:
                    dve.wait_ge(*sem_and_value)
                dve.tensor_scalar(rel[:, :], nodes, tile_lo[:, bass.ds(t, 1)], None, ALU.subtract).then_inc(s_dst_free, 1)
                dve.wait_ge(s_dst_free, r + 1)

            def chain(ps, t, k=0):
                return Chain(dve, s_td, t * STEPS[ps] + (done[ps] + TD0 + (CLEARS[ps] - STEPS[ps] if k else 0)))

            def clear_sums(ps, t):
                ch = chain(ps, t)
                ch.link(dve.memset(acc[0:TN, :], 0.0))
                if ps == 0:
                    ch.link(dve.memset(deg[0:TN, :], 0.0))
                assert ch.k == CLEARS[ps]

            def add_sums(ps, following):
                if ps == 0:
                    dve.wait_ge(s_used, following * SLOTS + SLOTS)
                    dve.tensor_tensor(deg[0:TN, :], deg[0:TN, :], p_deg[0:TN, 0:1], ALU.add).then_inc(s_deg, 1)
                    dve.wait_ge(s_deg, following)
                add_round(following, D)

            def aggregate(ps, t, base, *stage):
                def hots(q, r, first, stage=None):
                    relative(t, r, win_dst[:, :], (s_dstw, r * 16), (s_hot, r * SLOTS))
                    for j in range(SLOTS):
                        if j == CLOSE_AT:
                            opening = first and isinstance(t, int)
                            if not opening:
                                add_sums(ps, r)
                            if first:
                                if not opening:
                                    finish(ps, t)
                                clear_sums(ps, t)
                        if stage and j == TABLE_AT:
                            table_rows(*stage)
                        if stage and j == OWN_AT:
                            own_part(*stage)
                        dve.wait_ge(s_g[j], r * 16)
                        dve.tensor_scalar(hot[:, j, :], node_iota[:, :], rel[:, j:j + 1], slots[:, j, SC:SC + 2].bitcast(F32),
                                          ALU.is_equal, ALU.mult).then_inc(s_hot, 1)

                walk_rounds(dve, t, base, meta, hots, *stage)

            def mean_plus_state(t):
                return dve.scalar_tensor_tensor(out=y[0:TN, :], in0=acc[0:TN, :], scalar=inv_deg[0:TN, bass.ds(t, 1)],
                                                in1=tile_of(state, t), op0=ALU.mult, op1=ALU.add)

            STEPS = [4, 1, 3, 1]
            CLEARS = [2, 1, 1, 1]
            done = [sum(STEPS[:k]) * TILES for k in range(PASSES)]

            def finish(ps, following):
                ch = chain(ps, following, 1)
                tile = following - 1
                if ps == 0:
                    ch.link(dve.tensor_scalar(deg[0:TN, :], deg[0:TN, :], 1.0, None, ALU.max))
                    ch.link(dve.reciprocal(inv_deg[0:TN, bass.ds(tile, 1)], deg[0:TN, :]))
                if ps < LAYERS - 1:
                    dve.wait_ge(s_y_free, following + (ps + 1) * TILES)
                    mean_plus_state(tile).then_inc(s_y, 1)
                    dve.wait_ge(s_y, following + ps * TILES)
                else:
                    ch.link(mean_plus_state(tile))
                    dve.wait_ge(s_xt, following * 16 + 16 * TILES)
                    ch.link(dve.tensor_tensor(y[0:TN, :], y[0:TN, :], xt[0:TN, :], ALU.add))
                    dve.sem_inc(s_xt_free, 1)
                    *steps, normed = norm(following)
                    for step in steps:
                        step()
                    dve.wait_ge(s_tp, following + LAYERS * TILES)
                    dve.wait_ge(s_keep, following)
                    normed().then_inc(s_h, 1)
                    dve.wait_ge(s_h, following + LAYERS * TILES)
                assert ch.k == STEPS[ps] - CLEARS[ps]

            def finish_pass(ps):
                add_sums(ps, rounds_before(dve, ps + 1) + 1)
                finish(ps, TILES)

            for ps in range(LAYERS - 1):
                base = rounds_before(dve, ps)
                aggregate(ps, 0, base)
                with dve.Fori(1, TILES) as t:
                    aggregate(ps, t, base, (t + (ps + 1) * TILES, ps + 1, t - 1))
                finish_pass(ps)
                node((ps + 2) * TILES, ps + 1, TILES - 1)

            def norm(k):
                def sums():
                    dve.bn_stats(stats[0:TN, :], y[0:TN, :]).then_inc(s_bn, 1)

                def moments():
                    wait_alone(dve, s_bn, k)
                    dve.bn_aggr(mv[0:TN, :], stats[0:TN, :]).then_inc(s_mv, 1)

                def variance():
                    dve.wait_ge(s_mv, k)
                    dve.tensor_scalar(mv[0:TN, 1:2], mv[0:TN, 1:2], EPS, None, ALU.add).then_inc(s_var, 1)

                def normed():
                    dve.wait_ge(s_rstd, k * 2)
                    return dve.tensor_scalar(h_row[0:TN, :], y[0:TN, :], mv[0:TN, 0:1], rstd[0:TN, 0:1], ALU.subtract, ALU.mult)

                return sums, moments, variance, normed

            ps = LAYERS - 1
            base = rounds_before(dve, ps)
            dve.wait_ge(s_y_free, LAYERS * TILES + 1)
            aggregate(ps, 0, base)
            with dve.Fori(1, TILES) as t:
                aggregate(ps, t, base)
            finish_pass(ps)

            mch = Chain(dve, s_set_d, ch.k)
            flat = b2_row[:, :, :].rearrange("k a b -> k (a b)")
            part = [b2_part[:, k, :] for k in range(3)]
            for k in range(3):
                mch.link(dve.tensor_copy(part[k], flat))
                if k < 2:
                    mch.link(dve.tensor_tensor(flat, flat, part[k], ALU.subtract))
            parts = b2_parts[:, :, :].rearrange("k a b -> k (a b)")
            mch.link(dve.tensor_scalar(parts, part[0], ident[0:3, 0:1], None, ALU.mult))
            for k in range(1, 3):
                mch.link(dve.scalar_tensor_tensor(out=parts, in0=part[k], scalar=ident[0:3, k:k + 1], in1=parts, op0=ALU.mult, op1=ALU.add))
            mch.link(dve.memset(ones3[:, :], 1.0))

            def hidden(q):
                dve.wait_ge(s_mact, q * 6 + 6)
                dve.wait_ge(s_w, q * NG)
                rows = F * REST
                last = dve.scalar_tensor_tensor(out=filt_h[:, 0:FULL, :], in0=m_exp[:, 0:FULL, :], scalar=-LOG2,
                                                in1=m_relu[:, 0:FULL, :], op0=ALU.add, op1=ALU.add)
                if rows:
                    last = dve.scalar_tensor_tensor(out=filt_h[0:rows, FULL, :], in0=m_exp[0:rows, FULL, :], scalar=-LOG2,
                                                    in1=m_relu[0:rows, FULL, :], op0=ALU.add, op1=ALU.add)
                last.then_inc(s_mh, 1)

            def group(q, r, g):
                j0, n = GROUPS[g]
                if g not in ACT_HOTS:
                    dve.wait_ge(s_used, r * SLOTS + j0 + n)
                    dve.tensor_tensor(hot32[:, j0:j0 + n, :], node_iota32[:, :].unsqueeze(1).broadcast_to([P, n, TN]),
                                      rel[:, j0:j0 + n].unsqueeze(2).broadcast_to([P, n, TN]), ALU.is_equal)
                dve.wait_ge(s_w, q * NG + g + 1)
                for j in range(n):
                    dve.wait_ge(s_g[j0 + j], r * 16)
                dve.wait_ge(s_av2, q * NG + max(g - 1, 0))
                w = p_w[g % 2][:, 0:n * G].rearrange("p (j k f) -> p j k f", j=n, k=4)
                rows = msg_slots[:, j0:j0 + n, :]
                s = rows[:, :, 0:F]
                v = rows[:, :, F:G].rearrange("p j (c f) -> p j c f", c=C3)
                angle = y_cut[:, j0:j0 + n, 1:YD].unsqueeze(3).broadcast_to([P, n, C3, F])
                dve.tensor_tensor(av[:, g % 2, 0:n, 0:F], s, w[:, :, 0, :], ALU.mult)
                dve.tensor_tensor(av[:, g % 2, 0:n, F:G].rearrange("p j (c f) -> p j c f", c=C3), v,
                                  w[:, :, 3, :].unsqueeze(2).broadcast_to([P, n, C3, F]), ALU.mult).then_inc(s_av, 1)
                dve.tensor_tensor(vy[:, 0:n, :, :], v, angle, ALU.mult).then_inc(s_gd, 1)
                dve.wait_ge(s_m, q * NG + g)
                dve.tensor_tensor(ab[:, 0:n, :], s, w[:, :, 2, :], ALU.mult).then_inc(s_gd, 1)
                dve.wait_ge(s_gd, q * (3 * NG) + 3 * g + 1)
                dve.tensor_reduce(vys[:, 0:n, :], vy[:, 0:n, :, :].rearrange("p j c f -> p j f c"), AX.X, ALU.add).then_inc(s_gd, 1)
                dve.wait_ge(s_gd, q * (3 * NG) + 3 * g + 3)
                msg_free(dve, r, g)
                dve.scalar_tensor_tensor(out=msg[:, g % 2, 0:n, G:G + F], in0=vys[:, 0:n, :], scalar=IS3, in1=w[:, :, 1, :],
                                         op0=ALU.mult, op1=ALU.mult).then_inc(s_w_free, 1)
                dve.tensor_tensor(msg[:, g % 2, 0:n, G + F:2 * G].rearrange("p j (c f) -> p j c f", c=C3),
                                  ab[:, 0:n, :].unsqueeze(2).broadcast_to([P, n, C3, F]), angle, ALU.mult).then_inc(s_m, 1)

            def output_scalars(t):
                dve.wait_ge(s_oact, t * 3 + 3)
                dve.wait_ge(s_o2, t + 1)
                dve.scalar_tensor_tensor(out=o1[:, 0, :], in0=o_exp[:, :], scalar=-LOG2, in1=o_relu[:, :],
                                         op0=ALU.add, op1=ALU.add).then_inc(s_o1s, 1)

            def output(t):
                sums, moments, variance, normed = norm(t + TILES + 1)

                def residual():
                    dve.wait_ge(s_o2, t + 2)
                    rows = tile_of(state, t)
                    dve.scalar_tensor_tensor(out=y[0:TN, 0:B], in0=p_o2[0:TN, 0:B], scalar=RS_B, in1=rows[:, 0:B],
                                             op0=ALU.mult, op1=ALU.add)
                    dve.scalar_tensor_tensor(out=y[0:TN, B:D].rearrange("p (d c) -> p c d", c=C3),
                                             in0=p_o2[0:TN, B:D].rearrange("p (c d) -> p c d", c=C3), scalar=RS_B,
                                             in1=rows[:, B:D].rearrange("p (d c) -> p c d", c=C3), op0=ALU.mult, op1=ALU.add).then_inc(s_o2_free, 1)

                def stats_of_y():
                    dve.wait_ge(s_o2_free, t + 2)
                    sums()

                def store():
                    dve.wait_ge(s_outrow_free, t + 1)
                    normed().then_inc(s_out, 1)

                def moments_of_y():
                    moments()
                    variance()

                return residual, stats_of_y, moments_of_y, None, store

            def message_round(t, q, r, first, t_out=None, t_norm=None):
                relative(t, r, win_p[:, :, PAY_SRC].bitcast(I32), (s_src, r * 16), (s_m, q * NG), (s_h32, q * NH))
                dve.wait_ge(s_av2, q * NG)
                dve.tensor_tensor(y_cut[:, :, :], win_p[:, :, PAY_Y:PAY_Y + YD],
                                  win_p[:, :, PAY_C:PAY_C + 1].broadcast_to([P, SLOTS, YD]), ALU.mult).then_inc(s_yw_free, 1)
                dve.wait_ge(s_yw_free, q + 1)
                if isinstance(t, int) and t == 0 and first:
                    clear(0)
                else:
                    add_round(r, 2 * G)
                    if first:
                        close(t)
                        clear(t)
                steps = output(t_norm) if t_norm is not None else ()
                for g in range(NG):
                    group(q, r, g)
                    if steps and steps[g]:
                        steps[g]()
                hidden(q + 1)
                if t_out is not None:
                    output_scalars(t_out)

            def clear(t):
                dve.memset(acc[0:TN, 0:2 * G], 0.0).then_inc(s_td, 1)
                wait_alone(dve, s_td, t + (done[LAYERS] + TD0 + 1))

            def close(following):
                dve.wait_ge(s_ptp, following)
                dve.tensor_copy(pairs[0:TN, :, :].rearrange("p k (h f) -> p k h f", h=2),
                                acc[0:TN, 0:2 * G].rearrange("p (h k f) -> p k h f", h=2, k=4)).then_inc(s_pairs, 1)
                dve.wait_ge(s_pairs, following)

            ps = LAYERS
            base = rounds_before(dve, ps)
            dve.wait_ge(s_tp, (LAYERS + 1) * TILES + 1)
            dve.wait_ge(s_keep, TILES + 1)
            hidden(1)
            walk_rounds(dve, 0, base, meta_m, partial(message_round, 0))
            walk_rounds(dve, 1, base, meta_m, partial(message_round, 1), 0)
            with dve.Fori(2, TILES) as t:
                walk_rounds(dve, t, base, meta_m, partial(message_round, t), t - 1, t - 2)
            add_round(entry(dve, TILES, 0, 1, TILES * MAXR, meta_m) + base + 1, 2 * G)
            close(TILES)
            for step in filter(None, output(TILES - 2)):
                step()
            output_scalars(TILES - 1)
            for step in filter(None, output(TILES - 1)):
                step()



def kernel(x, src, dst, edge_attr_20, edge_attr_4, edge_weight, L0_gnn_Ws_self, L0_gnn_Ws_neigh, L0_gnn_bs,
           L1_gnn_w_in2f_s, L1_gnn_w_in2f_v, L1_gnn_W1, L1_gnn_b1, L1_gnn_W2, L1_gnn_b2,
           L1_gnn_w_f2o1_s, L1_gnn_w_f2o1_v, L1_gnn_w_f2o2_s, L1_gnn_w_f2o2_v):
    import numpy as np
    import concourse.bacc as bacc
    from concourse.bass_utils import run_bass_kernel_spmd

    def arr(a):
        return np.asarray(a)

    def padded(a, fill):
        a = arr(a)
        return np.concatenate([a, np.full((WIN,) + a.shape[1:], fill, a.dtype)])

    w2 = arr(L1_gnn_W2).reshape(F, F, 6)[:, :, 0:4].transpose(0, 2, 1).reshape(F, 4 * F)
    b2 = arr(L1_gnn_b2).reshape(F, 6)[:, 0:4].T.reshape(4 * F)
    wv = arr(L1_gnn_w_f2o1_v)
    pay = np.zeros((E + WIN, PAY), np.float32)
    pay[0:E, 0:PAY_Y] = arr(edge_attr_20)
    pay[0:E, PAY_Y:PAY_C] = arr(edge_attr_4)
    pay[0:E, PAY_C] = arr(edge_weight)
    pay.view(np.int32)[:, PAY_SRC] = padded(src, N)
    pay.view(np.int32)[:, PAY_DST] = padded(dst, 0)
    arrays = {
        "x": arr(x), "src": padded(src, 0), "dst": padded(dst, N),
        "src_n": padded(src, N)[0:P * CH], "pay": pay,
        "ws": arr(L0_gnn_Ws_self), "wn": arr(L0_gnn_Ws_neigh), "bs": arr(L0_gnn_bs),
        "w_in": np.stack([arr(L1_gnn_w_in2f_s), arr(L1_gnn_w_in2f_v)]),
        "w1": arr(L1_gnn_W1), "b1": arr(L1_gnn_b1), "w2": w2, "b2": b2,
        "wf1": np.stack([arr(L1_gnn_w_f2o1_s), np.concatenate([wv[F:], wv[:F]])]),
        "wf2": np.stack([arr(L1_gnn_w_f2o2_s), arr(L1_gnn_w_f2o2_v)]),
    }
    arrays = {k: np.ascontiguousarray(a) for k, a in arrays.items()}
    nc = bacc.Bacc("TRN2", target_bir_lowering=False, num_devices=1)
    aps = {k: nc.dram_tensor(k, a.shape, mybir.dt.from_np(a.dtype), kind="ExternalInput").ap() for k, a in arrays.items()}
    out = nc.dram_tensor("out", (N, D), F32, kind="ExternalOutput").ap()
    gnn_kernel(nc, out=out, **aps)
    r = run_bass_kernel_spmd(nc, [arrays], core_ids=[0])
    return r.results[0]["out"]
```
